# Optimizing a Trainium2 kernel written in Bass

```python
import numpy as np
import jax
import jax.numpy as jnp

def _softmax(x, axis=-1):
    return jax.nn.softmax(x, axis=axis)

def _gelu(x):
    return jax.nn.gelu(x, approximate=True)

def _silu(x):
    return jax.nn.silu(x)

def _sigmoid(x):
    return jax.nn.sigmoid(x)

def _layernorm(x, axis=-1, eps=1e-05):
    m = jnp.mean(x, axis=axis, keepdims=True)
    v = jnp.var(x, axis=axis, keepdims=True)
    return (x - m) / jnp.sqrt(v + eps)

def _scatter_add(tgt, idx, src, axis=0):
    return tgt.at[idx].add(src)

def _segment_sum(src, seg, n):
    return jax.ops.segment_sum(src, seg, n)
kernel_name = 'mk_seq_postln_d1_jaxref_r4_c571bc'

def setup_inputs(seed: int=0):
    np.random.seed(seed)
    _w = jnp.asarray

    def _L0_attn_setup():
        import jax, jax.numpy as jnp
        import numpy as np
        import math
        B, S, DM, H, F = (2, 512, 256, 16, 192)
        DH = F // 3
        MAX_BIAS = 8.0

        def _get_slopes(n):

            def pow2(n):
                start = 2.0 ** (-2.0 ** (-(math.log2(n) - 3)))
                return [start * start ** i for i in range(n)]
            if math.log2(n).is_integer():
                return pow2(n)
            cp2 = 2 ** math.floor(math.log2(n))
            return pow2(cp2) + _get_slopes(2 * cp2)[0::2][:n - cp2]

        def _rope_sin_cos(seq_len, dim):
            inv_freq = 1.0 / 10000.0 ** (jnp.arange(0, dim, 2, dtype=jnp.float32) / dim)
            freqs = jnp.outer(jnp.arange(seq_len, dtype=jnp.float32), inv_freq)
            sin = jnp.concatenate([jnp.sin(freqs), jnp.sin(freqs)], axis=-1)
            cos = jnp.concatenate([jnp.cos(freqs), jnp.cos(freqs)], axis=-1)
            return (sin, cos)

        def _rotate_half(x):
            x1, x2 = jnp.split(x, 2, axis=-1)
            return jnp.concatenate([-x2, x1], axis=-1)
        key = jax.random.key(seed)
        kx, kq, ko = jax.random.split(key, 3)
        x = jax.random.normal(kx, (B, S, DM), dtype=jnp.float32)
        w_qkv = jax.random.normal(kq, (DM, H, F), dtype=jnp.float32) * (1.0 / math.sqrt(DM))
        b_qkv = jnp.zeros((H, F), dtype=jnp.float32)
        w_out = jax.random.normal(ko, (H, DH, DM), dtype=jnp.float32) * (1.0 / math.sqrt(H * DH))
        b_out = jnp.zeros((DM,), dtype=jnp.float32)
        return {'x': x, 'w_qkv': w_qkv, 'b_qkv': b_qkv, 'w_out': w_out, 'b_out': b_out}
    _L0_attn_in = _L0_attn_setup()

    def _L0_ffn_setup():
        import jax, jax.numpy as jnp
        import numpy as np
        D_IN, D_HID = (256, 1024)

        def _ternary(key, shape):
            return jax.random.randint(key, shape, -1, 2).astype(jnp.float32)

        def _tlin(x, w, s):
            return jnp.einsum('bsi,oi->bso', x, w) * s
        key = jax.random.key(seed)
        ks = jax.random.split(key, 12)
        inv = lambda fan: 1.0 / np.sqrt(fan).astype(np.float32)
        return {'x': jax.random.normal(ks[0], (4, 512, D_IN), dtype=jnp.float32), 'w1_w': _ternary(ks[1], (D_HID, D_IN)), 'w1_s': jax.random.uniform(ks[2], (D_HID,), dtype=jnp.float32) * inv(D_IN), 'w2_w': _ternary(ks[3], (D_HID, D_IN)), 'w2_s': jax.random.uniform(ks[4], (D_HID,), dtype=jnp.float32) * inv(D_IN), 'h1_w': _ternary(ks[5], (D_HID, D_HID)), 'h1_s': jax.random.uniform(ks[6], (D_HID,), dtype=jnp.float32) * inv(D_HID), 'h2_w': _ternary(ks[7], (D_HID, D_HID)), 'h2_s': jax.random.uniform(ks[8], (D_HID,), dtype=jnp.float32) * inv(D_HID), 'w3_w': _ternary(ks[9], (D_IN, D_HID)), 'w3_s': jax.random.uniform(ks[10], (D_IN,), dtype=jnp.float32) * inv(D_HID)}
    _L0_ffn_in = _L0_ffn_setup()
    _d = {'L0_attn_x': _L0_attn_in['x'], 'L0_attn_w_qkv': _L0_attn_in['w_qkv'], 'L0_attn_b_qkv': _L0_attn_in['b_qkv'], 'L0_attn_w_out': _L0_attn_in['w_out'], 'L0_attn_b_out': _L0_attn_in['b_out'], 'L0_ffn_w1_w': _L0_ffn_in['w1_w'], 'L0_ffn_w1_s': _L0_ffn_in['w1_s'], 'L0_ffn_w2_w': _L0_ffn_in['w2_w'], 'L0_ffn_w2_s': _L0_ffn_in['w2_s'], 'L0_ffn_h1_w': _L0_ffn_in['h1_w'], 'L0_ffn_h1_s': _L0_ffn_in['h1_s'], 'L0_ffn_h2_w': _L0_ffn_in['h2_w'], 'L0_ffn_h2_s': _L0_ffn_in['h2_s'], 'L0_ffn_w3_w': _L0_ffn_in['w3_w'], 'L0_ffn_w3_s': _L0_ffn_in['w3_s']}
    _x0 = _d['L0_attn_x']
    _d['L0_attn_x'] = jax.random.normal(jax.random.fold_in(jax.random.key(seed), 1), (2, 2048, 256), dtype=_x0.dtype)
    del _x0
    return _d

def reference(L0_attn_x, L0_attn_w_qkv, L0_attn_b_qkv, L0_attn_w_out, L0_attn_b_out, L0_ffn_w1_w, L0_ffn_w1_s, L0_ffn_w2_w, L0_ffn_w2_s, L0_ffn_h1_w, L0_ffn_h1_s, L0_ffn_h2_w, L0_ffn_h2_s, L0_ffn_w3_w, L0_ffn_w3_s):

    def _L0_attn_ref(x, w_qkv, b_qkv, w_out, b_out):
        import jax, jax.numpy as jnp
        import numpy as np
        import math
        B, S, DM, H, F = (2, 512, 256, 16, 192)
        DH = F // 3
        MAX_BIAS = 8.0

        def _get_slopes(n):

            def pow2(n):
                start = 2.0 ** (-2.0 ** (-(math.log2(n) - 3)))
                return [start * start ** i for i in range(n)]
            if math.log2(n).is_integer():
                return pow2(n)
            cp2 = 2 ** math.floor(math.log2(n))
            return pow2(cp2) + _get_slopes(2 * cp2)[0::2][:n - cp2]

        def _rope_sin_cos(seq_len, dim):
            inv_freq = 1.0 / 10000.0 ** (jnp.arange(0, dim, 2, dtype=jnp.float32) / dim)
            freqs = jnp.outer(jnp.arange(seq_len, dtype=jnp.float32), inv_freq)
            sin = jnp.concatenate([jnp.sin(freqs), jnp.sin(freqs)], axis=-1)
            cos = jnp.concatenate([jnp.cos(freqs), jnp.cos(freqs)], axis=-1)
            return (sin, cos)

        def _rotate_half(x):
            x1, x2 = jnp.split(x, 2, axis=-1)
            return jnp.concatenate([-x2, x1], axis=-1)
        b, s, dm = x.shape
        h, f = (w_qkv.shape[1], w_qkv.shape[2])
        dh = f // 3
        qkv = jnp.einsum('bsd,dhf->bshf', x, w_qkv) + b_qkv
        q, k, v = jnp.split(qkv, 3, axis=-1)
        sin, cos = _rope_sin_cos(s, dh)
        sin, cos = (sin[:, None, :], cos[:, None, :])
        q = q * cos + _rotate_half(q) * sin
        k = k * cos + _rotate_half(k) * sin
        q = q.transpose(0, 2, 1, 3)
        k = k.transpose(0, 2, 1, 3)
        v = v.transpose(0, 2, 1, 3)
        scores = jnp.einsum('bhqd,bhkd->bhqk', q, k) / jnp.sqrt(jnp.float32(f))
        slopes = jnp.asarray(_get_slopes(h), dtype=jnp.float32)
        pos = jnp.arange(s, dtype=jnp.float32)
        rel = pos[None, :] - pos[:, None]
        rel = jnp.where(rel > 0, 0.0, rel)
        alibi = rel[None, :, :] * slopes[:, None, None] * MAX_BIAS
        scores = scores + alibi[None]
        causal = jnp.tril(jnp.ones((s, s), dtype=jnp.float32))
        scores = jnp.where(causal == 0, -1000000000.0, scores)
        weights = jax.nn.softmax(scores, axis=-1)
        attn = jnp.einsum('bhqk,bhkd->bhqd', weights, v).transpose(0, 2, 1, 3)
        return jnp.einsum('bshd,hdm->bsm', attn, w_out) + b_out

    def _L0_ffn_ref(x, w1_w, w1_s, w2_w, w2_s, h1_w, h1_s, h2_w, h2_s, w3_w, w3_s):
        import jax, jax.numpy as jnp
        import numpy as np
        D_IN, D_HID = (256, 1024)

        def _ternary(key, shape):
            return jax.random.randint(key, shape, -1, 2).astype(jnp.float32)

        def _tlin(x, w, s):
            return jnp.einsum('bsi,oi->bso', x, w) * s
        h = jax.nn.silu(_tlin(x, w1_w, w1_s)) * _tlin(x, w2_w, w2_s)
        h = jax.nn.gelu(_tlin(h, h1_w, h1_s), approximate=False)
        h = jax.nn.gelu(_tlin(h, h2_w, h2_s), approximate=False)
        return _tlin(h, w3_w, w3_s)
    x = L0_attn_x
    x = _layernorm(x + _L0_attn_ref(x, L0_attn_w_qkv, L0_attn_b_qkv, L0_attn_w_out, L0_attn_b_out), axis=-1)
    x = _layernorm(x + _L0_ffn_ref(x, L0_ffn_w1_w, L0_ffn_w1_s, L0_ffn_w2_w, L0_ffn_w2_s, L0_ffn_h1_w, L0_ffn_h1_s, L0_ffn_h2_w, L0_ffn_h2_s, L0_ffn_w3_w, L0_ffn_w3_s), axis=-1)
    return x

_drawn_inputs = setup_inputs


def setup_inputs(seed=0):
    import zlib

    import numpy as np

    out = dict(_drawn_inputs(seed))
    spreads = {'L0_attn_b_qkv': (0.0, 0.1), 'L0_attn_b_out': (0.0, 0.1)}
    factors = {'L0_ffn_w1_w': 8.0,
     'L0_ffn_w1_s': 8.0,
     'L0_ffn_w2_w': 8.0,
     'L0_ffn_w2_s': 8.0,
     'L0_ffn_h1_w': 8.0,
     'L0_ffn_h1_s': 8.0,
     'L0_ffn_h2_w': 8.0,
     'L0_ffn_h2_s': 8.0,
     'L0_ffn_w3_w': 8.0,
     'L0_ffn_w3_s': 8.0}
    for name, (base, spread) in spreads.items():
        noise = np.random.default_rng([zlib.crc32(name.encode()), seed]).standard_normal(out[name].shape)
        drawn = base * np.exp(spread * noise) if base else spread * noise
        out[name] = jnp.asarray(drawn.astype(out[name].dtype))
    for name, factor in factors.items():
        out[name] = (out[name] * factor).astype(out[name].dtype)
    return out
```

```python
from contextlib import ExitStack

import concourse.bass as bass
from concourse import mybir

F32 = mybir.dt.float32
F32R = mybir.dt.float32r
F16 = mybir.dt.float16
ALU = mybir.AluOpType
ACT = mybir.ActivationFunctionType

P = 128
B, S, DM, H, DH = 2, 2048, 256, 16, 64
KD = DM // P
NT = S // P
PAIRS = H // 2
PAIR_COLS = 2 * 3 * DH
QK_COLS = 2 * 2 * DH
HALF = DH // 2
Q_SCALE = -1.0 / float(3 * DH) ** 0.5
BANK = 512
S_CHUNK = 2 * BANK
NEG_MASK = 1.0e12

ORDER = [t for g in range(NT // 4) for t in (NT - 2 - 2 * g, NT - 1 - 2 * g, 2 * g, 2 * g + 1)]
TILES = 2 * NT
GROUPS = TILES // 2
HEAD_OF = [j // NT for j in range(TILES)]
TILE_OF = [ORDER[j % NT] for j in range(TILES)]

D_HID = 1024
MT = D_HID // P
TOK = 1024
CHUNKS = B * S // TOK
TT = TOK // P
EPS = 1e-5


def hold(eng, passed):
    eng.sem_inc(passed, 1)


def s_chunks(j):
    width = P * (TILE_OF[j] + 1)
    return [(c, min(S_CHUNK, width - c)) for c in range(0, width, S_CHUNK)]


def t_chunks(j):
    n = TILE_OF[j] + 1
    return [(k, min(4, n - k)) for k in range(0, n, 4)]


S_SUM = [sum(len(s_chunks(i)) for i in range(j)) for j in range(TILES + 1)]
T_SUM = [sum(len(t_chunks(i)) for i in range(j)) for j in range(TILES + 1)]


def attention(nc, ins, attn_dram):
    ctx = ExitStack()
    with ctx:
        def sb(name, shape, dt=F32):
            return ctx.enter_context(nc.sbuf_tensor(name, shape, dt))

        def sem(name):
            return ctx.enter_context(nc.semaphore(name))

        x_hi = sb("x_hi", [P, KD, S], F32R)
        x_lo = sb("x_lo", [P, KD, S], F32R)
        rel = sb("rel", [P, S], F16)
        mask = sb("mask", [P, P])
        bias_t = sb("bias_t", [P, S])
        k_hi = sb("k_hi", [P, 2, S], F32R)
        k_lo = sb("k_lo", [P, 2, S], F32R)
        q_st = sb("q_st", [P, 2, S], F32R)
        v_st = sb("v_st", [P, 2, NT, 2 * DH], F32R)
        long_rows = sb("long_rows", [P, 2, S])
        short_rows = sb("short_rows", [P, 2, S // 2])
        pt_long_hi = sb("pt_long_hi", [P, NT, 2 * P], F32R)
        pt_long_lo = sb("pt_long_lo", [P, NT, 2 * P], F32R)
        pt_short_hi = sb("pt_short_hi", [P, NT // 2, 2 * P], F32R)
        pt_short_lo = sb("pt_short_lo", [P, NT // 2, 2 * P], F32R)
        o_sb = sb("o_sb", [P, 2, 2 * P])
        o_nat = sb("o_nat", [P, 2, 2, DH])
        cos = sb("cos", [P, NT, HALF])
        sin = sb("sin", [P, NT, DH])
        w_raw = sb("w_raw", [P, KD, PAIR_COLS])
        w_hi = sb("w_hi", [P, KD, PAIR_COLS], F32R)
        w_lo = sb("w_lo", [P, KD, PAIR_COLS], F32R)
        b_raw = sb("b_raw", [DH, PAIR_COLS])
        b_hi = sb("b_hi", [DH, PAIR_COLS], F32R)
        b_st = sb("b_st", [P, PAIR_COLS], F32R)
        ones = sb("ones", [P, P], F32R)
        ident = sb("ident", [P, P])
        fold = sb("fold", [P, DH])
        slopes = sb("slopes", [P, 48])
        row_min = sb("row_min", [P, TILES, 2])
        row_sum = sb("row_sum", [P, TILES])
        row_inv = sb("row_inv", [P, TILES])

        work = long_rows[:, :, :].rearrange("p a s -> p (a s)")
        proj = work[:, 0:3 * PAIR_COLS].rearrange("p (n c) -> p n c", n=3)
        at = 3 * PAIR_COLS
        by_cos = work[:, at:at + 2 * QK_COLS].rearrange("p (n c) -> p n c", n=2)
        at += 2 * QK_COLS
        by_sin = work[:, at:at + 2 * QK_COLS].rearrange("p (n c) -> p n c", n=2)
        at += 2 * QK_COLS
        roped = work[:, at:at + 4 * QK_COLS].rearrange("p (n h r d) -> p n h r d", n=2, h=4, r=2)

        def rows_of(j):
            t = TILE_OF[j]
            return (long_rows if t >= NT // 2 else short_rows)[:, t % 2, :]

        def pt_of(q):
            return (pt_long_hi, pt_long_lo) if q % 2 == 0 else (pt_short_hi, pt_short_lo)

        ps_s = ctx.enter_context(nc.psum_tensor("ps_s", [P, 2, S_CHUNK], F32))
        ps_t = ctx.enter_context(nc.psum_tensor("ps_t", [P, 2, BANK], F32))
        ps_o = ctx.enter_context(nc.psum_tensor("ps_o", [P, BANK], F32))
        ps_n = ctx.enter_context(nc.psum_tensor("ps_n", [P, BANK], F32))

        consts_loaded = sem("consts_loaded")
        ones_ready = sem("ones_ready")
        x_loaded = sem("x_loaded")
        x_hi_ready = sem("x_hi_ready")
        x_lo_ready = sem("x_lo_ready")
        w_loaded = sem("w_loaded")
        w_hi_ready = sem("w_hi_ready")
        w_split = sem("w_split")
        proj_done = sem("proj_done")
        proj_copied = sem("proj_copied")
        v_hi_ready = sem("v_hi_ready")
        v_lo_ready = sem("v_lo_ready")
        rope_mul = sem("rope_mul")
        rope_add = sem("rope_add")
        qk_turned = sem("qk_turned")
        qk_hi_ready = sem("qk_hi_ready")
        qk_lo_ready = sem("qk_lo_ready")
        bias_built = sem("bias_built")
        bias_masked = sem("bias_masked")
        scored = sem("scored")
        biased = sem("biased")
        exped = sem("exped")
        pt_turned = sem("pt_turned")
        pt_hi_ready = sem("pt_hi_ready")
        pt_lo_ready = sem("pt_lo_ready")
        pt_zeroed = sem("pt_zeroed")
        pv_done = sem("pv_done")
        o_copied = sem("o_copied")
        folded = sem("folded")
        inverted = sem("inverted")
        normed = sem("normed")
        stored = [sem("stored_even"), sem("stored_odd")]

        sp_passed, pool_passed, dve_passed, pe_passed = (sem(f"{e}_passed") for e in ("sp", "pool", "dve", "pe"))

        n_consts = 7
        S_ALL, T_ALL = S_SUM[TILES], T_SUM[TILES]
        BIAS_PER = 3
        LOW = 6 * P
        block = ctx.enter_context(nc.Block())

        @block.sync
        def _(sp):
            for dst, src in ((ident, "ident"), (fold, "fold"), (cos, "cos"), (sin, "sin"),
                             (rel, "rel"), (mask, "mask"), (slopes, "slopes")):
                sp.dma_start(dst[:], ins[src]).then_inc(consts_loaded, 16)

            def load_w(pair):
                sp.dma_start(w_raw[:], ins["w_qkv"][pair]).then_inc(w_loaded, 16)
                sp.dma_start(b_raw[0:1, :], ins["b_qkv"][pair]).then_inc(w_loaded, 16)
                sp.dma_start(b_raw[32:33, :], ins["b_qkv"][pair]).then_inc(w_loaded, 16)

            sp.wait_ge(ones_ready, 1)
            load_w(0)
            with sp.Fori(0, B) as b:
                sp.dma_start(long_rows[:, :, :], ins["x_t"][b]).then_inc(x_loaded, 16)
                with sp.Fori(0, PAIRS) as p:
                    it = b * PAIRS + p
                    sp.wait_ge(w_split, it + 1)
                    load_w(p + 1)
                    for q in range(GROUPS):
                        sp.wait_ge(normed, it * GROUPS + q + 1)
                        hold(sp, sp_passed)
                        first = TILE_OF[2 * q]
                        dst = attn_dram[b, first:first + 2, :, 2 * p + HEAD_OF[2 * q], :]
                        sp.dma_start(dst.rearrange("t p d -> p t d"), o_nat[:, q % 2, :, :]) \
                            .then_inc(stored[q % 2], 16)
                    sp.wait_ge(pt_turned, (it + 1) * T_ALL)
                    hold(sp, sp_passed)
            for par in range(2):
                sp.wait_ge(stored[par], 16 * (B * PAIRS * GROUPS // 2 + 1))
            sp.wait_ge(w_loaded, 48 * (B * PAIRS + 1))

        @block.gpsimd
        def _(pool):
            pool.memset(b_raw[:], 0.0)
            pool.memset(b_st[:].bitcast(F32), 0.0)
            pool.memset(ones[:].bitcast(F32), 0.0)
            pool.drain()
            pool.memset(ones[0:1, :].bitcast(F32), 1.0)
            pool.drain()
            pool.memset(ones[32:33, :].bitcast(F32), 1.0).then_inc(ones_ready, 1)

            def split_w(lots):
                pool.wait_ge(w_loaded, lots * 48)
                hold(pool, pool_passed)
                pool.tensor_copy(w_hi[:], w_raw[:])
                pool.tensor_copy(b_hi[:], b_raw[:])
                pool.tensor_copy(b_st[0:1, :], b_raw[0:1, :]).then_inc(w_hi_ready, 1)
                pool.wait_ge(w_hi_ready, lots * 2 - 1)
                pool.tensor_tensor(w_lo[:], w_raw[:], w_hi[:].bitcast(F32), ALU.subtract).then_inc(w_hi_ready, 1)
                pool.wait_ge(w_hi_ready, lots * 2)
                pool.tensor_tensor(b_st[32:33, :], b_raw[32:33, :], b_hi[32:33, :].bitcast(F32),
                                   ALU.subtract).then_inc(w_split, 1)
                pool.wait_ge(w_split, lots)
                hold(pool, pool_passed)

            pool.wait_ge(ones_ready, 1)
            split_w(1)
            pool.wait_ge(consts_loaded, 16 * n_consts)
            with pool.Fori(0, B * PAIRS) as it:
                for t in range(NT):
                    pool.wait_ge(proj_copied, it * NT + t + 1)
                    if t >= 2:
                        pool.wait_ge(rope_add, it * NT + t - 1)
                    src = proj[:, t % 3, 0:QK_COLS].rearrange("p (h r d) -> p h r d", h=4, r=2)
                    cos_t = cos[:, t, :].rearrange("p (a b d) -> p a b d", a=1, b=1)
                    pool.tensor_tensor(by_cos[:, t % 2, :].rearrange("p (h r d) -> p h r d", h=4, r=2),
                                       src, cos_t.to_broadcast([P, 4, 2, HALF]), ALU.mult)
                    for r in range(2):
                        sin_t = sin[:, t, r * HALF:(r + 1) * HALF].rearrange("p (a d) -> p a d", a=1)
                        out = by_sin[:, t % 2, :].rearrange("p (h r d) -> p h r d", h=4, r=2)[:, :, r, :]
                        last = pool.tensor_tensor(out, src[:, :, 1 - r, :],
                                                  sin_t.to_broadcast([P, 4, HALF]), ALU.mult)
                    last.then_inc(rope_mul, 1)
                    pool.wait_ge(v_hi_ready, it * NT + t + 1)
                    pool.tensor_tensor(v_st[:, :, t, DH:2 * DH],
                                       proj[:, t % 3, QK_COLS:PAIR_COLS].rearrange("p (h d) -> p h d", h=2),
                                       v_st[:, :, t, 0:DH].bitcast(F32), ALU.subtract).then_inc(v_lo_ready, 1)
                pool.wait_ge(proj_done, (it + 1) * NT)
                split_w(it + 2)
                for q in range(GROUPS):
                    last_key = TILE_OF[2 * q] + 1
                    if q >= 2:
                        pool.wait_ge(pv_done, it * GROUPS + q - 1)
                        hold(pool, pool_passed)
                    hi, lo = pt_of(q)
                    pool.memset(hi[:, last_key, 0:P].bitcast(F32), 0.0)
                    pool.memset(lo[:, last_key, 0:P].bitcast(F32), 0.0).then_inc(pt_zeroed, 1)

        @block.scalar
        def _(act):
            act.wait_ge(consts_loaded, 16 * n_consts)

            def build_bias(it, head, lo, hi):
                act.activation(bias_t[:, lo:hi], rel[:, lo:hi], ACT.Copy,
                               scale=slopes[:, bass.ds(it * 2 + head, 1)]).then_inc(bias_built, 1)

            act.preload_act_table(ACT.Exp)
            with act.Fori(0, B * PAIRS, PAIRS) as b0:
                act.wait_ge(x_loaded, b0 * 2 + 16)
                act.activation(x_hi[:], long_rows[:, :, :], ACT.Copy).then_inc(x_hi_ready, PAIRS)
                with act.Fori(b0, b0 + PAIRS) as it:
                    for step in range(NT + 2):
                        t = step
                        if t < NT:
                            act.wait_ge(proj_done, it * NT + t + 1)
                            if t == 0:
                                act.wait_ge(x_lo_ready, b0 + PAIRS)
                            if t >= 3:
                                act.wait_ge(rope_mul, it * NT + t - 2)
                                act.wait_ge(v_lo_ready, it * NT + t - 2)
                            act.activation(proj[:, t % 3, :], ps_s[:, t % 2, 0:PAIR_COLS], ACT.Copy) \
                                .then_inc(proj_copied, 1)
                            act.wait_ge(proj_copied, it * NT + t + 1)
                            act.activation(v_st[:, :, t, 0:DH],
                                           proj[:, t % 3, QK_COLS:PAIR_COLS].rearrange("p (h d) -> p h d", h=2),
                                           ACT.Copy).then_inc(v_hi_ready, 1)
                            if t == 0:
                                build_bias(it, 0, 0, S)
                        t = step - 2
                        if t >= 0:
                            act.wait_ge(qk_turned, it * NT + t + 1)
                            turned = ps_t[:, t % 2, :].rearrange("p (h c) -> p h c", h=4)
                            act.activation(q_st[:, :, t * P:(t + 1) * P], turned[:, 0:2, :], ACT.Copy,
                                           scale=Q_SCALE)
                            act.activation(k_hi[:, :, t * P:(t + 1) * P], turned[:, 2:4, :], ACT.Copy) \
                                .then_inc(qk_hi_ready, 1)

                    def exp(j):
                        width = P * (TILE_OF[j] + 1)
                        act.wait_ge(biased, it * S_ALL + S_SUM[j + 1])
                        rows = rows_of(j)[:, 0:width]
                        n = len(s_chunks(j)) - 1
                        act.activation(rows, rows, ACT.Exp, bias=row_min[:, j, n:n + 1], scale=-1.0,
                                       accum_out=row_sum[:, j:j + 1]).then_inc(exped, 1)

                    def pt_high(j, c):
                        k0, n = t_chunks(j)[c]
                        i = T_SUM[j] + c
                        q = j // 2
                        if c == 0 and q >= 2:
                            act.wait_ge(pv_done, it * GROUPS + q - 1)
                        act.wait_ge(pt_turned, it * T_ALL + i + 1)
                        act.activation(pt_of(q)[0][:, k0:k0 + n, (j % 2) * P:(j % 2 + 1) * P],
                                       ps_t[:, i % 2, 0:n * P].rearrange("p (k c) -> p k c", k=n),
                                       ACT.Copy).then_inc(pt_hi_ready, 1)

                    exp(0)
                    for j in range(TILES + 3):
                        if j >= 4 and j % 2 == 0:
                            q = (j - 4) // 2
                            act.wait_ge(pv_done, it * GROUPS + q + 1)
                            if q >= 2:
                                act.wait_ge(folded, it * GROUPS + q - 1)
                            act.activation(o_sb[:, q % 2, :], ps_o[:, 0:2 * P], ACT.Copy).then_inc(o_copied, 1)
                        if j < TILES:
                            n = len(t_chunks(j))
                            for c in range(min(2, n)):
                                pt_high(j, c)
                            if j + 1 < TILES:
                                exp(j + 1)
                            if j == 9:
                                act.wait_ge(biased, it * S_ALL + S_SUM[10])
                                build_bias(it, 1, 0, LOW)
                            if j == 14:
                                build_bias(it, 1, LOW, S)
                            for c in range(2, n):
                                pt_high(j, c)

        @block.vector
        def _(dve):
            for par in range(2):
                dve.memset(o_nat[:, par, :, :], 0.0).then_inc(stored[par], 16)
            dve.wait_ge(consts_loaded, 16 * n_consts)
            with dve.Fori(0, B * PAIRS, PAIRS) as b0:
                dve.wait_ge(x_hi_ready, b0 + PAIRS)
                dve.tensor_tensor(x_lo[:], long_rows[:, :, :], x_hi[:].bitcast(F32), ALU.subtract) \
                    .then_inc(x_lo_ready, PAIRS)
                with dve.Fori(b0, b0 + PAIRS) as it:
                    def mask_bias(n):
                        dve.wait_ge(bias_built, it * BIAS_PER + n)
                        dve.tensor_tensor(bias_t[:, S - P:S], bias_t[:, S - P:S], mask[:], ALU.add) \
                            .then_inc(bias_masked, 1)

                    for step in range(NT + 2):
                        t = step - 1
                        if 0 <= t < NT:
                            dve.wait_ge(rope_mul, it * NT + t + 1)
                            if t >= 2:
                                dve.wait_ge(qk_turned, it * NT + t - 1)
                            shape = [P, 4, 2, DH]
                            dve.tensor_tensor(
                                roped[:, t % 2],
                                by_cos[:, t % 2, :].rearrange("p (h r d) -> p h r d", h=4, r=1).to_broadcast(shape),
                                by_sin[:, t % 2, :].rearrange("p (h r d) -> p h r d", h=4, r=1).to_broadcast(shape),
                                ALU.add).then_inc(rope_add, 1)
                        t = step - 2
                        if t == 1:
                            mask_bias(1)
                        if t >= 0:
                            dve.wait_ge(qk_hi_ready, it * NT + t + 1)
                            turned = ps_t[:, t % 2, :].rearrange("p (h c) -> p h c", h=4)
                            cols = slice(t * P, (t + 1) * P)
                            dve.scalar_tensor_tensor(q_st[DH:P, :, cols], turned[DH:P, 0:2, :], Q_SCALE,
                                                     q_st[DH:P, :, cols].bitcast(F32), ALU.mult, ALU.subtract)
                            dve.tensor_tensor(k_lo[:, :, cols], turned[:, 2:4, :],
                                              k_hi[:, :, cols].bitcast(F32), ALU.subtract) \
                                .then_inc(qk_lo_ready, 1)

                    def add_bias(j):
                        if j == NT:
                            mask_bias(3)
                        for c, (k0, width) in enumerate(s_chunks(j)):
                            i = S_SUM[j] + c
                            if c == 0:
                                if j >= 4:
                                    dve.wait_ge(pt_turned, it * T_ALL + T_SUM[j - 3])
                                dve.wait_ge(bias_masked, it * 2 + HEAD_OF[j] + 1)
                            else:
                                dve.wait_ge(biased, it * S_ALL + i)
                            dve.wait_ge(scored, it * S_ALL + i + 1)
                            hold(dve, dve_passed)
                            off = S - P - P * TILE_OF[j] + k0
                            dve.tensor_tensor_reduce(
                                rows_of(j)[:, k0:k0 + width], ps_s[:, i % 2, 0:width], bias_t[:, off:off + width],
                                1.0, 3.0e38 if c == 0 else row_min[:, j, 0:1], ALU.add, ALU.min,
                                row_min[:, j, c:c + 1]).then_inc(biased, 1)

                    def pt_low(j, c):
                        k0, n = t_chunks(j)[c]
                        i = T_SUM[j] + c
                        hi, lo = pt_of(j // 2)
                        cols = slice((j % 2) * P, (j % 2 + 1) * P)
                        dve.wait_ge(pt_hi_ready, it * T_ALL + i + 1)
                        dve.tensor_tensor(lo[:, k0:k0 + n, cols],
                                          ps_t[:, i % 2, 0:n * P].rearrange("p (k c) -> p k c", k=n),
                                          hi[:, k0:k0 + n, cols].bitcast(F32), ALU.subtract) \
                            .then_inc(pt_lo_ready, 1)

                    dve.wait_ge(v_lo_ready, (it + 1) * NT)
                    add_bias(0)
                    add_bias(1)
                    for j in range(TILES + 5):
                        if j >= 6 and j % 2 == 0:
                            q = (j - 6) // 2
                            dve.wait_ge(exped, it * TILES + 2 * q + 2)
                            dve.reciprocal(row_inv[:, 2 * q:2 * q + 2], row_sum[:, 2 * q:2 * q + 2]) \
                                .then_inc(inverted, 1)
                            dve.wait_ge(folded, it * GROUPS + q + 1)
                            dve.wait_ge(stored[q % 2], (it * (GROUPS // 2) + q // 2 + 1) * 16)
                            dve.wait_ge(inverted, it * GROUPS + q + 1)
                            inv = row_inv[:, 2 * q:2 * q + 2].rearrange("p (t a) -> p t a", a=1)
                            dve.tensor_tensor(o_nat[:, q % 2, :, :],
                                              ps_n[:, 0:2 * DH].rearrange("p (t d) -> p t d", t=2),
                                              inv.to_broadcast([P, 2, DH]), ALU.mult).then_inc(normed, 1)
                        if j < TILES:
                            n = len(t_chunks(j))
                            for c in range(min(2, n)):
                                pt_low(j, c)
                            if j + 2 < TILES:
                                add_bias(j + 2)
                            for c in range(2, n):
                                pt_low(j, c)

        @block.tensor
        def _(pe):
            pe.wait_ge(consts_loaded, 16 * n_consts)
            pe.wait_ge(ones_ready, 1)
            with pe.Fori(0, B * PAIRS, PAIRS) as b0:
                pe.wait_ge(x_hi_ready, b0 + PAIRS)
                pe.wait_ge(x_lo_ready, b0 + PAIRS)
                hold(pe, pe_passed)
                with pe.Fori(b0, b0 + PAIRS) as it:
                    pe.wait_ge(w_split, it + 1)
                    for step in range(NT + 2):
                        t = step
                        if t < NT:
                            if t >= 2:
                                pe.wait_ge(proj_copied, it * NT + t - 1)
                            out = ps_s[:, t % 2, 0:PAIR_COLS]
                            rows = slice(t * P, (t + 1) * P)
                            pe.matmul(out, ones[:], b_st[:], start=True, stop=False)
                            for k in range(KD):
                                pe.matmul(out, x_hi[:, k, rows], w_hi[:, k, :], start=False, stop=False)
                                pe.matmul(out, x_hi[:, k, rows], w_lo[:, k, :], start=False, stop=False)
                                last = pe.matmul(out, x_lo[:, k, rows], w_hi[:, k, :], start=False,
                                                 stop=k == KD - 1)
                            last.then_inc(proj_done, 1)
                        t = step - 2
                        if t >= 0:
                            pe.wait_ge(rope_add, it * NT + t + 1)
                            if t >= 2:
                                pe.wait_ge(qk_lo_ready, it * NT + t - 1)
                            for h in range(4):
                                src = roped[:, t % 2, h].rearrange("p r d -> p (r d)")
                                last = pe.transpose(ps_t[:, t % 2, h * P:(h + 1) * P], src, ident[:])
                            last.then_inc(qk_turned, 1)

                    def score(j):
                        head, rows = HEAD_OF[j], slice(TILE_OF[j] * P, (TILE_OF[j] + 1) * P)
                        for c, (k0, width) in enumerate(s_chunks(j)):
                            i = S_SUM[j] + c
                            if i >= 2:
                                pe.wait_ge(biased, it * S_ALL + i - 1)
                            for n0 in range(0, width, BANK):
                                n = max(2 * P, min(BANK, width - n0))
                                keys = slice(k0 + n0, k0 + n0 + n)
                                out = ps_s[:, i % 2, n0:n0 + n]
                                pe.matmul(out, q_st[:, head, rows], k_hi[:, head, keys], start=True, stop=False)
                                last = pe.matmul(out, q_st[:, head, rows], k_lo[:, head, keys],
                                                 start=False, stop=True)
                            last.then_inc(scored, 1)

                    def turn(j, c):
                        k0, n = t_chunks(j)[c]
                        i = T_SUM[j] + c
                        if i >= 2:
                            pe.wait_ge(pt_lo_ready, it * T_ALL + i - 1)
                        if c == 0:
                            pe.wait_ge(exped, it * TILES + j + 1)
                        for k in range(n):
                            last = pe.transpose(ps_t[:, i % 2, k * P:(k + 1) * P],
                                                rows_of(j)[:, (k0 + k) * P:(k0 + k + 1) * P], ident[:])
                        last.then_inc(pt_turned, 1)

                    def weigh(q, half):
                        keys = TILE_OF[2 * q] + 2
                        head = HEAD_OF[2 * q]
                        hi, lo = pt_of(q)
                        if half == 0:
                            pe.wait_ge(pt_lo_ready, it * T_ALL + T_SUM[2 * q + 2])
                            pe.wait_ge(pt_zeroed, it * GROUPS + q + 1)
                            if q >= 1:
                                pe.wait_ge(o_copied, it * GROUPS + q)
                        for k in range(half * keys // 2, (half + 1) * keys // 2):
                            for part in (hi, lo):
                                last = pe.matmul(ps_o[:, 0:2 * P], v_st[:, head, k, :], part[:, k, :],
                                                 start=k == 0 and part is hi, stop=k == keys - 1 and part is lo)
                        if half:
                            last.then_inc(pv_done, 1)

                    def add_parts(q):
                        pe.wait_ge(o_copied, it * GROUPS + q + 1)
                        if q >= 1:
                            pe.wait_ge(normed, it * GROUPS + q)
                        for r in range(2):
                            last = pe.matmul(ps_n[:, r * DH:(r + 1) * DH], o_sb[:, q % 2, r * P:(r + 1) * P],
                                             fold[:], start=True, stop=True)
                        last.then_inc(folded, 1)

                    pe.wait_ge(proj_copied, (it + 1) * NT)
                    pe.wait_ge(v_lo_ready, (it + 1) * NT)
                    pe.wait_ge(qk_lo_ready, (it + 1) * NT)
                    score(0)
                    score(1)
                    for j in range(TILES + 4):
                        n = len(t_chunks(j)) if j < TILES else 0
                        for c in range(min(2, n)):
                            turn(j, c)
                        if j + 2 < TILES:
                            score(j + 2)
                        if j >= 5 and j % 2 == 1:
                            add_parts((j - 5) // 2)
                        if 2 <= j < TILES + 2:
                            weigh((j - 2) // 2, j % 2)
                        for c in range(2, n):
                            turn(j, c)
                    pe.wait_ge(biased, (it + 1) * S_ALL)
                    pe.wait_ge(pt_lo_ready, (it + 1) * T_ALL)
                    pe.wait_ge(normed, (it + 1) * GROUPS)
                    hold(pe, pe_passed)


SLABS = 2 + MT // 2 + 2 * MT + 2
SLAB = 1024
SLAB_UP, SLAB_HID, SLAB_DOWN = 2, 2 + MT // 2, 2 + MT // 2 + 2 * MT
HALVES = TOK // BANK


def feed_forward(nc, ins, attn_dram, out):
    ctx = ExitStack()
    with ctx:
        def sb(name, shape, dt=F32):
            return ctx.enter_context(nc.sbuf_tensor(name, shape, dt))

        def sem(name):
            return ctx.enter_context(nc.semaphore(name))

        slab_raw = sb("slab_raw", [P, 2, SLAB])
        slab_hi = sb("slab_hi", [P, 2, SLAB], F32R)
        slab_lo = sb("slab_lo", [P, 2, SLAB], F32R)
        attn = sb("attn", [P, 2, H * DH])
        y_nat = sb("y_nat", [P, TT, DM])
        y_hi = sb("y_hi", [P, KD, TOK], F32R)
        y_lo = sb("y_lo", [P, KD, TOK], F32R)
        ha_hi = sb("ha_hi", [P, MT, TOK], F32R)
        ha_lo = sb("ha_lo", [P, MT, TOK], F32R)
        hb_hi = sb("hb_hi", [P, MT, TOK], F32R)
        hb_lo = sb("hb_lo", [P, MT, TOK], F32R)
        silu = sb("silu", [P, 2, BANK])
        hid = sb("hid", [P, 2, BANK])
        ident = sb("ident_f", [P, P])
        s_hid = sb("s_hid", [P, 4, MT])
        b_out = sb("b_out", [P, DM])
        s_down = sb("s_down", [P, DM])
        eps = sb("eps", [P, 1])
        stats = sb("stats", [P, TT, 6])
        moments = sb("moments", [P, TT, 2])
        std = sb("std", [P, TT])
        rstd = sb("rstd", [P, TT])

        ps_m = ctx.enter_context(nc.psum_tensor("ps_m", [P, 4, BANK], F32))
        ps_acc = ctx.enter_context(nc.psum_tensor("ps_acc", [P, TT, DM], F32))

        consts_loaded = sem("f_consts_loaded")
        eps_ready = sem("eps_ready")
        raw_loaded = [sem("raw_loaded_even"), sem("raw_loaded_odd")]
        slab_hi_ready = sem("slab_hi_ready")
        slab_ready = sem("slab_ready")
        slab_used = sem("slab_used")
        x_loaded = sem("f_x_loaded")
        attn_loaded = [sem("attn_loaded_even"), sem("attn_loaded_odd")]
        x_biased = sem("x_biased")
        attn_turned = sem("attn_turned")
        attn_hi_ready = sem("attn_hi_ready")
        attn_lo_ready = sem("attn_lo_ready")
        acc_done = sem("acc_done")
        step_done = sem("step_done")
        var_ready = sem("var_ready")
        std_ready = sem("std_ready")
        y_ready = sem("y_ready")
        y_turned = sem("y_turned")
        y_hi_ready = sem("y_hi_ready")
        y_lo_ready = sem("y_lo_ready")
        up_done = sem("up_done")
        silu_ready = sem("silu_ready")
        gated = sem("gated")
        up_hi_ready = sem("up_hi_ready")
        up_lo_ready = sem("up_lo_ready")
        hid_done = sem("hid_done")
        gelu_ready = sem("gelu_ready")
        hid_hi_ready = sem("hid_hi_ready")
        hid_lo_ready = sem("hid_lo_ready")
        out_ready = sem("out_ready")
        out_stored = sem("out_stored")

        sp_passed, pool_passed, dve_passed, pe_passed = (sem(f"f_{e}_passed") for e in ("sp", "pool", "dve", "pe"))

        tokens = "(c t p) d -> c p t d"
        x_rows = ins["x"].rearrange("b s d -> (b s) d").rearrange(tokens, t=TT, p=P)
        out_rows = out.rearrange("b s d -> (b s) d").rearrange(tokens, t=TT, p=P)
        attn_rows = attn_dram.rearrange("b t p h d -> (b t) p (h d)").rearrange("(c t) p d -> c t p d", t=TT)
        UP_UNITS = MT * HALVES
        HID_UNITS = 2 * MT * HALVES
        CHAIN = 3 * TT + 2 * (TT + 1)
        n_consts = 4

        def hid_place(n):
            return n // UP_UNITS, n % UP_UNITS // HALVES, slice(n % HALVES * BANK, (n % HALVES + 1) * BANK)

        block = ctx.enter_context(nc.Block())

        @block.sync
        def _(sp):
            sp.dma_start(ident[:], ins["ident"]).then_inc(consts_loaded, 16)
            sp.dma_start(s_hid[:], ins["s_hid"]).then_inc(consts_loaded, 16)
            sp.dma_start(b_out[:], ins["b_out"].to_broadcast([P, DM])).then_inc(consts_loaded, 16)
            sp.dma_start(s_down[:], ins["s_down"].to_broadcast([P, DM])).then_inc(consts_loaded, 16)
            for s in range(2):
                sp.dma_start(slab_raw[:, s, :], ins["slabs"][s]).then_inc(raw_loaded[s], 16)
            with sp.Fori(0, CHUNKS) as c:
                sp.dma_start(y_nat[:], x_rows[c]).then_inc(x_loaded, 16)
                for s in range(SLABS):
                    sp.wait_ge(slab_ready, c * SLABS + s + 1)
                    sp.dma_start(slab_raw[:, s % 2, :], ins["slabs"][(s + 2) % SLABS]) \
                        .then_inc(raw_loaded[s % 2], 16)
                sp.wait_ge(out_ready, c * TT + TT)
                sp.dma_start(out_rows[c], y_nat[:]).then_inc(out_stored, 16)
                sp.wait_ge(out_stored, c * 16 + 16)
                hold(sp, sp_passed)
            sp.wait_ge(out_stored, CHUNKS * 16)
            for par in range(2):
                sp.wait_ge(raw_loaded[par], 16 * (CHUNKS * SLABS // 2 + 1))

        @block.gpsimd
        def _(pool):
            pool.memset(eps[:], EPS).then_inc(eps_ready, 1)

            def split(s, loads, lots):
                pool.wait_ge(raw_loaded[s % 2], loads * 16)
                hold(pool, pool_passed)
                pool.tensor_copy(slab_hi[:, s % 2, :], slab_raw[:, s % 2, :]).then_inc(slab_hi_ready, 1)
                pool.wait_ge(slab_hi_ready, lots)
                pool.tensor_tensor(slab_lo[:, s % 2, :], slab_raw[:, s % 2, :],
                                   slab_hi[:, s % 2, :].bitcast(F32), ALU.subtract).then_inc(slab_ready, 1)

            split(0, 1, 1)
            split(1, 1, 2)
            pool.wait_ge(consts_loaded, 16 * n_consts)
            with pool.Fori(0, CHUNKS) as c:
                pool.wait_ge(x_loaded, c * 16 + 16)
                for t in range(TT):
                    last = pool.tensor_tensor(y_nat[:, t, :], y_nat[:, t, :], b_out[:], ALU.add)
                    last.then_inc(x_biased, 1)
                for s in range(SLABS):
                    pool.wait_ge(slab_used, c * SLABS + s + 1)
                    split(s, c * (SLABS // 2) + s // 2 + 2, c * SLABS + s + 3)

        @block.scalar
        def _(act):
            def load_attn(c, t):
                act.dma_start(attn[:, t % 2, :], attn_rows[c, t]).then_inc(attn_loaded[t % 2], 16)

            act.wait_ge(eps_ready, 1)
            act.wait_ge(consts_loaded, 16 * n_consts)
            with act.Fori(0, CHUNKS) as c:
                load_attn(c, 0)
                load_attn(c, 1)
                for u in range(2 * TT):
                    t, k0 = u // 2, u % 2 * 4
                    act.wait_ge(attn_turned, c * 2 * TT + u + 1)
                    act.activation(hb_hi[:, k0:k0 + 4, t * P:(t + 1) * P],
                                   ps_m[:, u % 4, :].rearrange("p (k c) -> p k c", k=4), ACT.Copy) \
                        .then_inc(attn_hi_ready, 1)
                    if u % 2 and t + 2 < TT:
                        load_attn(c, t + 2)

                def sqrt(n):
                    act.wait_ge(var_ready, (c * 2 + n) * TT)
                    act.activation(std[:], moments[:, :, 1], ACT.Sqrt, bias=eps[:]).then_inc(std_ready, 1)

                sqrt(1)
                for u in range(TT // 2):
                    act.wait_ge(y_turned, c * (TT // 2) + u + 1)
                    act.activation(y_hi[:, :, u * 2 * P:(u + 1) * 2 * P].rearrange("p k (t c) -> p t k c", t=2),
                                   ps_m[:, u % 4, :].rearrange("p (t k c) -> p t k c", t=2, k=KD), ACT.Copy) \
                        .then_inc(y_hi_ready, 1)
                for n in range(UP_UNITS + 1):
                    if n < UP_UNITS:
                        act.wait_ge(up_done, c * UP_UNITS + n + 1)
                        if n >= 2:
                            act.wait_ge(gated, c * UP_UNITS + n - 1)
                        act.activation(silu[:, n % 2, :], ps_m[:, n % 2 * 2, :], ACT.Silu,
                                       scale=s_hid[:, 0, n // HALVES:n // HALVES + 1]).then_inc(silu_ready, 1)
                    if n >= 1:
                        m, cols = (n - 1) // HALVES, slice((n - 1) % HALVES * BANK, ((n - 1) % HALVES + 1) * BANK)
                        act.wait_ge(gated, c * UP_UNITS + n)
                        act.activation(ha_hi[:, m, cols], hid[:, (n - 1) % 2, :], ACT.Copy).then_inc(up_hi_ready, 1)
                for n in range(HID_UNITS):
                    layer, m, cols = hid_place(n)
                    act.wait_ge(hid_done, c * HID_UNITS + n + 1)
                    if n >= 2:
                        act.wait_ge(hid_lo_ready, c * HID_UNITS + n - 1)
                    act.activation(hid[:, n % 2, :], ps_m[:, n % 4, :], ACT.Gelu,
                                   scale=s_hid[:, 2 + layer, m:m + 1]).then_inc(gelu_ready, 1)
                    act.wait_ge(gelu_ready, c * HID_UNITS + n + 1)
                    act.activation((ha_hi if layer else hb_hi)[:, m, cols], hid[:, n % 2, :], ACT.Copy) \
                        .then_inc(hid_hi_ready, 1)
                sqrt(2)

        @block.vector
        def _(dve):
            dve.wait_ge(consts_loaded, 16 * n_consts)
            with dve.Fori(0, CHUNKS) as c:
                for u in range(2 * TT):
                    t, k0 = u // 2, u % 2 * 4
                    dve.wait_ge(attn_hi_ready, c * 2 * TT + u + 1)
                    dve.tensor_tensor(hb_lo[:, k0:k0 + 4, t * P:(t + 1) * P],
                                      ps_m[:, u % 4, :].rearrange("p (k c) -> p k c", k=4),
                                      hb_hi[:, k0:k0 + 4, t * P:(t + 1) * P].bitcast(F32), ALU.subtract) \
                        .then_inc(attn_lo_ready, 1)

                steps = [0]

                def chained(op):
                    steps[0] += 1
                    op.then_inc(step_done, 1)

                def wait_chain(back=0):
                    dve.wait_ge(step_done, c * CHAIN + steps[0] - back)

                def layernorm(n, ready):
                    for t in range(TT):
                        chained(dve.bn_stats(stats[:, t, :], y_nat[:, t, :]))
                    for t in range(TT):
                        wait_chain(TT - 1 - t)
                        hold(dve, dve_passed)
                        dve.bn_aggr(moments[:, t, :], stats[:, t, :]).then_inc(var_ready, 1)
                    dve.wait_ge(std_ready, c * 2 + n)
                    chained(dve.reciprocal(rstd[:], std[:]))
                    wait_chain()
                    for t in range(TT):
                        dve.tensor_scalar(y_nat[:, t, :], y_nat[:, t, :], moments[:, t, 0:1], rstd[:, t:t + 1],
                                          ALU.subtract, ALU.mult).then_inc(ready, 1)

                for t in range(TT):
                    dve.wait_ge(x_biased, c * TT + t + 1)
                    dve.wait_ge(acc_done, c * 2 * TT + (t | 1) + 1)
                    chained(dve.tensor_tensor(y_nat[:, t, :], ps_acc[:, t, :], y_nat[:, t, :], ALU.add))
                wait_chain()
                layernorm(1, y_ready)
                for u in range(TT // 2):
                    dve.wait_ge(y_hi_ready, c * (TT // 2) + u + 1)
                    view = lambda a: a[:, :, u * 2 * P:(u + 1) * 2 * P].rearrange("p k (t c) -> p t k c", t=2)
                    dve.tensor_tensor(view(y_lo), ps_m[:, u % 4, :].rearrange("p (t k c) -> p t k c", t=2, k=KD),
                                      view(y_hi).bitcast(F32), ALU.subtract).then_inc(y_lo_ready, 1)
                for n in range(UP_UNITS + 1):
                    if n < UP_UNITS:
                        m = n // HALVES
                        if n >= 2:
                            dve.wait_ge(up_lo_ready, c * UP_UNITS + n - 1)
                        dve.wait_ge(silu_ready, c * UP_UNITS + n + 1)
                        dve.scalar_tensor_tensor(hid[:, n % 2, :], ps_m[:, n % 2 * 2 + 1, :], s_hid[:, 1, m:m + 1],
                                                 silu[:, n % 2, :], ALU.mult, ALU.mult).then_inc(gated, 1)
                    if n >= 1:
                        m, cols = (n - 1) // HALVES, slice((n - 1) % HALVES * BANK, ((n - 1) % HALVES + 1) * BANK)
                        dve.wait_ge(up_hi_ready, c * UP_UNITS + n)
                        dve.tensor_tensor(ha_lo[:, m, cols], hid[:, (n - 1) % 2, :], ha_hi[:, m, cols].bitcast(F32),
                                          ALU.subtract).then_inc(up_lo_ready, 1)
                for n in range(HID_UNITS):
                    layer, m, cols = hid_place(n)
                    dve.wait_ge(hid_hi_ready, c * HID_UNITS + n + 1)
                    dve.tensor_tensor((ha_lo if layer else hb_lo)[:, m, cols], hid[:, n % 2, :],
                                      (ha_hi if layer else hb_hi)[:, m, cols].bitcast(F32),
                                      ALU.subtract).then_inc(hid_lo_ready, 1)
                for t in range(TT):
                    dve.wait_ge(acc_done, c * 2 * TT + TT + (t | 1) + 1)
                    chained(dve.tensor_tensor(silu[:, t % 2, 0:DM], ps_acc[:, t, :], s_down[:], ALU.mult))
                    wait_chain()
                    chained(dve.tensor_tensor(y_nat[:, t, :], silu[:, t % 2, 0:DM], y_nat[:, t, :], ALU.add))
                wait_chain()
                layernorm(2, out_ready)
                assert steps[0] == CHAIN, steps[0]

        @block.tensor
        def _(pe):
            pe.wait_ge(consts_loaded, 16 * n_consts)
            with pe.Fori(0, CHUNKS) as c:
                for u in range(2 * TT):
                    t, k0 = u // 2, u % 2 * 4
                    if u % 2 == 0:
                        pe.wait_ge(attn_loaded[t % 2], (c * (TT // 2) + t // 2 + 1) * 16)
                    if u >= 4:
                        pe.wait_ge(attn_lo_ready, c * 2 * TT + u - 3)
                    for k in range(4):
                        last = pe.transpose(ps_m[:, u % 4, k * P:(k + 1) * P],
                                            attn[:, t % 2, (k0 + k) * P:(k0 + k + 1) * P], ident[:])
                    last.then_inc(attn_turned, 1)

                def rows_out(first, hi, lo):
                    for half in range(2):
                        s = first + half
                        pe.wait_ge(slab_ready, c * SLABS + s + 1)
                        for t in range(TT):
                            for kk in range(4):
                                k = half * 4 + kk
                                wh = slab_hi[:, s % 2, kk * DM:(kk + 1) * DM]
                                wl = slab_lo[:, s % 2, kk * DM:(kk + 1) * DM]
                                rows = slice(t * P, (t + 1) * P)
                                pe.matmul(ps_acc[:, t, :], hi[:, k, rows], wh, start=k == 0 and t % 2 == 0,
                                          stop=False, skip_group_check=True)
                                pe.matmul(ps_acc[:, t, :], hi[:, k, rows], wl, start=False, stop=False,
                                          skip_group_check=True)
                                last = pe.matmul(ps_acc[:, t, :], lo[:, k, rows], wh, start=False,
                                                 stop=k == MT - 1, skip_group_check=True)
                            if half:
                                last.then_inc(acc_done, 1)
                        pe.drain().then_inc(slab_used, 1)

                pe.wait_ge(attn_lo_ready, (c + 1) * 2 * TT)
                rows_out(0, hb_hi, hb_lo)
                for u in range(TT // 2):
                    pe.wait_ge(y_ready, c * TT + 2 * u + 2)
                    for t in range(2):
                        for k in range(KD):
                            last = pe.transpose(ps_m[:, u % 4, (t * KD + k) * P:(t * KD + k + 1) * P],
                                                y_nat[:, 2 * u + t, k * P:(k + 1) * P], ident[:])
                    last.then_inc(y_turned, 1)
                pe.wait_ge(y_lo_ready, (c + 1) * (TT // 2))

                def product(out, s, at, hi, lo, cols, tiles):
                    for k in range(tiles):
                        wh = slab_hi[:, s % 2, at + k * P:at + (k + 1) * P]
                        wl = slab_lo[:, s % 2, at + k * P:at + (k + 1) * P]
                        pe.matmul(out, wh, hi[:, k, cols], start=k == 0, stop=False)
                        pe.matmul(out, wh, lo[:, k, cols], start=False, stop=False)
                        last = pe.matmul(out, wl, hi[:, k, cols], start=False, stop=k == tiles - 1)
                    return last

                for n in range(UP_UNITS):
                    m, cols = n // HALVES, slice(n % HALVES * BANK, (n % HALVES + 1) * BANK)
                    s = SLAB_UP + m // 2
                    if n % (2 * HALVES) == 0:
                        pe.wait_ge(slab_ready, c * SLABS + s + 1)
                    if n >= 2:
                        pe.wait_ge(gated, c * UP_UNITS + n - 1)
                    for w in range(2):
                        last = product(ps_m[:, n % 2 * 2 + w, :], s, (m % 2 * 2 + w) * KD * P, y_hi, y_lo, cols, KD)
                    last.then_inc(up_done, 1)
                    if n % (2 * HALVES) == 2 * HALVES - 1:
                        pe.drain().then_inc(slab_used, 1)
                pe.wait_ge(up_lo_ready, (c + 1) * UP_UNITS)
                for n in range(HID_UNITS):
                    layer, m, cols = hid_place(n)
                    s = SLAB_HID + layer * MT + m
                    if n % HALVES == 0:
                        pe.wait_ge(slab_ready, c * SLABS + s + 1)
                    if n == UP_UNITS:
                        pe.wait_ge(hid_lo_ready, c * HID_UNITS + UP_UNITS)
                    elif n >= 4:
                        pe.wait_ge(gelu_ready, c * HID_UNITS + n - 3)
                    hi, lo = (hb_hi, hb_lo) if layer else (ha_hi, ha_lo)
                    product(ps_m[:, n % 4, :], s, 0, hi, lo, cols, MT).then_inc(hid_done, 1)
                    if n % HALVES == HALVES - 1:
                        pe.drain().then_inc(slab_used, 1)
                pe.wait_ge(hid_lo_ready, (c + 1) * HID_UNITS)
                rows_out(SLAB_DOWN, ha_hi, ha_lo)
                pe.wait_ge(out_ready, (c + 1) * TT)
                hold(pe, pe_passed)


def program(nc, ins, out):
    attn_dram = nc.dram_tensor("attn_scratch", (B, NT, P, H, DH), F32, kind="Internal").ap()
    attention(nc, ins, attn_dram)
    feed_forward(nc, ins, attn_dram, out)


def _constants():
    import numpy as np

    pos = np.arange(S, dtype=np.float32)
    inv_freq = (1.0 / np.float32(10000.0) ** (np.arange(0, DH, 2, dtype=np.float32) / np.float32(DH))).astype(np.float32)
    freqs = np.outer(pos, inv_freq).astype(np.float32)
    rows = lambda a: np.ascontiguousarray(a.reshape(NT, P, -1).transpose(1, 0, 2)).astype(np.float32)
    start = 2.0 ** (-8.0 / H)
    slope = np.array([start ** (h + 1) for h in range(H)], np.float32) * np.float32(8.0)
    slopes = np.zeros(48, np.float32)
    slopes[0:2 * H] = np.tile(slope, 2)
    dist = np.arange(P)[:, None] - (np.arange(S)[None, :] - (S - P))
    return {
        "ident": np.eye(P, dtype=np.float32),
        "fold": np.concatenate([np.eye(DH, dtype=np.float32)] * 2),
        "cos": rows(np.cos(freqs)),
        "sin": rows(np.concatenate([-np.sin(freqs), np.sin(freqs)], axis=1)),
        "rel": np.maximum(dist, 0).astype(np.float16),
        "mask": np.where(dist[:, S - P:] < 0, np.float32(NEG_MASK), np.float32(0)).astype(np.float32),
        "slopes": np.ascontiguousarray(np.broadcast_to(slopes, (P, 48))),
    }


def kernel(L0_attn_x, L0_attn_w_qkv, L0_attn_b_qkv, L0_attn_w_out, L0_attn_b_out, L0_ffn_w1_w, L0_ffn_w1_s,
           L0_ffn_w2_w, L0_ffn_w2_s, L0_ffn_h1_w, L0_ffn_h1_s, L0_ffn_h2_w, L0_ffn_h2_s, L0_ffn_w3_w, L0_ffn_w3_s):
    import numpy as np
    import concourse.bacc as bacc
    from concourse.bass_utils import run_bass_kernel_spmd

    c = np.ascontiguousarray
    a = lambda v: np.asarray(v)

    def by_pair(w):
        w = w.reshape(w.shape[0], PAIRS, 2, 3, DH).transpose(1, 0, 3, 2, 4).reshape(PAIRS, w.shape[0], PAIR_COLS)
        return np.concatenate([w, w[0:1]])

    w_qkv = by_pair(a(L0_attn_w_qkv)).reshape(PAIRS + 1, KD, P, PAIR_COLS).transpose(0, 2, 1, 3)
    rows_k = lambda w: w.reshape(2, 4, P, DM).transpose(0, 2, 1, 3).reshape(2, P, SLAB)
    cols_m = lambda w: w.reshape(MT, P, -1, P).transpose(0, 3, 2, 1)
    up = np.stack([cols_m(a(L0_ffn_w1_w)), cols_m(a(L0_ffn_w2_w))], axis=2)
    up = up.reshape(MT // 2, 2, P, 2, KD, P).transpose(0, 2, 1, 3, 4, 5).reshape(MT // 2, P, SLAB)
    slabs = np.concatenate([
        rows_k(a(L0_attn_w_out).reshape(H * DH, DM)), up,
        cols_m(a(L0_ffn_h1_w)).reshape(MT, P, SLAB), cols_m(a(L0_ffn_h2_w)).reshape(MT, P, SLAB),
        rows_k(a(L0_ffn_w3_w).T),
    ])
    scales = np.stack([a(s).reshape(MT, P) for s in (L0_ffn_w1_s, L0_ffn_w2_s, L0_ffn_h1_s, L0_ffn_h2_s)])
    arrays = _constants() | {
        "x": a(L0_attn_x),
        "x_t": a(L0_attn_x).transpose(0, 2, 1).reshape(B, KD, P, S).transpose(0, 2, 1, 3),
        "w_qkv": w_qkv,
        "b_qkv": by_pair(a(L0_attn_b_qkv).reshape(1, H * 3 * DH)),
        "slabs": slabs,
        "s_hid": scales.transpose(2, 0, 1),
        "b_out": a(L0_attn_b_out).reshape(1, DM),
        "s_down": a(L0_ffn_w3_s).reshape(1, DM),
    }
    nc = bacc.Bacc("TRN2", target_bir_lowering=False, num_devices=1)
    feed, ins = {}, {}
    for name, v in arrays.items():
        feed[f"in_{name}"] = c(v)
        ins[name] = nc.dram_tensor(f"in_{name}", v.shape, mybir.dt.from_np(v.dtype), kind="ExternalInput").ap()
    out = nc.dram_tensor("out_rows", (B, S, DM), F32, kind="ExternalOutput").ap()
    program(nc, ins, out)
    return run_bass_kernel_spmd(nc, [feed], core_ids=[0]).results[0]["out_rows"]
```

```python
from contextlib import ExitStack

import concourse.bass as bass
from concourse import mybir

F32 = mybir.dt.float32
F32R = mybir.dt.float32r
F16 = mybir.dt.float16
ALU = mybir.AluOpType
ACT = mybir.ActivationFunctionType

P = 128
B, S, DM, H, DH = 2, 2048, 256, 16, 64
KD = DM // P
NT = S // P
PAIRS = H // 2
PAIR_COLS = 2 * 3 * DH
QK_COLS = 2 * 2 * DH
HALF = DH // 2
Q_SCALE = -1.0 / float(3 * DH) ** 0.5
BANK = 512
NEG_MASK = 1.0e12

ORDER = [t for g in range(NT // 4) for t in (NT - 2 - 2 * g, NT - 1 - 2 * g, 2 * g, 2 * g + 1)]
AHEAD = 3
TILES = 2 * NT
GROUPS = TILES // 2
HEAD_OF = [j // NT for j in range(TILES)]
TILE_OF = [ORDER[j % NT] for j in range(TILES)]

D_HID = 1024
MT = D_HID // P
TOK = 1024
CHUNKS = B * S // TOK
TT = TOK // P
EPS = 1e-5


PIECE = 512
PIECES = 3


def hold(eng, passed):
    eng.sem_inc(passed, 1)


def s_chunks(j):
    width = P * (TILE_OF[j] + 1)
    return [(c, min(BANK, width - c)) for c in range(0, width, BANK)]


def t_chunks(j):
    n = TILE_OF[j] + 1
    return [(k, min(4, n - k)) for k in range(0, n, 4)]


S_SUM = [sum(len(s_chunks(i)) for i in range(j)) for j in range(TILES + 1)]
T_SUM = [sum(len(t_chunks(i)) for i in range(j)) for j in range(TILES + 1)]


def attention(nc, ins, attn_dram, lo_max):
    ctx = ExitStack()
    with ctx:
        def sb(name, shape, dt=F32):
            return ctx.enter_context(nc.sbuf_tensor(name, shape, dt))

        def sem(name):
            return ctx.enter_context(nc.semaphore(name))

        x_hi = sb("x_hi", [P, KD, S], F32R)
        x_lo = sb("x_lo", [P, KD, S], F32R)
        rel = sb("rel", [P, S], F16)
        mask = sb("mask", [P, P])
        bias_t = sb("bias_t", [P, S])
        k_hi = sb("k_hi", [P, 2, S], F32R)
        k_lo = sb("k_lo", [P, 2, S], F32R)
        q_st = sb("q_st", [P, 2, S], F32R)
        v_st = sb("v_st", [P, 2, NT, 2 * DH], F32R)
        long_rows = sb("long_rows", [P, 2, S])
        short_rows = sb("short_rows", [P, 2, S // 2])
        pt_long_hi = sb("pt_long_hi", [P, NT, 2 * P], F32R)
        pt_long_lo = sb("pt_long_lo", [P, NT, 2 * P], F32R)
        pt_short_hi = sb("pt_short_hi", [P, NT // 2, 2 * P], F32R)
        pt_short_lo = sb("pt_short_lo", [P, NT // 2, 2 * P], F32R)
        o_sb = sb("o_sb", [P, 2, 2 * P])
        o_nat = sb("o_nat", [P, 2, 2, DH])
        cos = sb("cos", [P, NT, HALF])
        sin = sb("sin", [P, NT, DH])
        w_raw = sb("w_raw", [P, KD, PAIR_COLS])
        w_hi = sb("w_hi", [P, KD, PAIR_COLS], F32R)
        w_lo = sb("w_lo", [P, KD, PAIR_COLS], F32R)
        b_raw = sb("b_raw", [DH, PAIR_COLS])
        b_hi = sb("b_hi", [DH, PAIR_COLS], F32R)
        b_st = sb("b_st", [P, PAIR_COLS], F32R)
        ones = sb("ones", [P, P], F32R)
        ident = sb("ident", [P, P])
        fold = sb("fold", [P, DH])
        slopes = sb("slopes", [P, 48])
        row_min = sb("row_min", [P, TILES, 4])
        row_sum = sb("row_sum", [P, TILES])
        row_inv = sb("row_inv", [P, TILES])

        piece, piece_hi, piece_lo = (w[:, :, :].rearrange("p k c -> p (k c)")[:, 0:PIECE]
                                     for w in (w_raw, w_hi, w_lo))

        work = long_rows[:, :, :].rearrange("p a s -> p (a s)")
        proj = work[:, 0:3 * PAIR_COLS].rearrange("p (n c) -> p n c", n=3)
        at = 3 * PAIR_COLS
        by_cos = work[:, at:at + 2 * QK_COLS].rearrange("p (n c) -> p n c", n=2)
        at += 2 * QK_COLS
        by_sin = work[:, at:at + 2 * QK_COLS].rearrange("p (n c) -> p n c", n=2)
        at += 2 * QK_COLS
        roped = work[:, at:at + 4 * QK_COLS].rearrange("p (n h r d) -> p n h r d", n=2, h=4, r=2)

        def rows_of(j):
            t = TILE_OF[j]
            return (long_rows if t >= NT // 2 else short_rows)[:, t % 2, :]

        def pt_of(q):
            return (pt_long_hi, pt_long_lo) if q % 2 == 0 else (pt_short_hi, pt_short_lo)

        ps_s = ctx.enter_context(nc.psum_tensor("ps_s", [P, 3, BANK], F32))
        ps_t = ctx.enter_context(nc.psum_tensor("ps_t", [P, 3, BANK], F32))
        ps_o = ctx.enter_context(nc.psum_tensor("ps_o", [P, 2, BANK], F32))
        ps_v, ps_n = ps_o[:, :, 0:2 * P], ps_o[:, :, 2 * P:3 * P]

        consts_loaded = sem("consts_loaded")
        ones_ready = sem("ones_ready")
        x_loaded = sem("x_loaded")
        x_hi_ready = sem("x_hi_ready")
        x_lo_ready = sem("x_lo_ready")
        w_loaded = sem("w_loaded")
        w_hi_ready = sem("w_hi_ready")
        w_split = sem("w_split")
        piece_loaded = sem("piece_loaded")
        piece_split = sem("piece_split")
        piece_done = sem("piece_done")
        proj_done = sem("proj_done")
        proj_copied = sem("proj_copied")
        v_hi_ready = sem("v_hi_ready")
        v_lo_ready = sem("v_lo_ready")
        rope_mul = sem("rope_mul")
        rope_add = sem("rope_add")
        qk_turned = sem("qk_turned")
        qk_hi_ready = sem("qk_hi_ready")
        qk_lo_ready = sem("qk_lo_ready")
        bias_built = sem("bias_built")
        bias_masked = sem("bias_masked")
        scored = sem("scored")
        biased = sem("biased")
        exped = sem("exped")
        pt_turned = sem("pt_turned")
        pt_hi_ready = sem("pt_hi_ready")
        pt_lo_ready = sem("pt_lo_ready")
        pt_zeroed = sem("pt_zeroed")
        pv_done = sem("pv_done")
        o_copied = sem("o_copied")
        folded = sem("folded")
        inverted = sem("inverted")
        normed = sem("normed")
        stored = [sem("stored_even"), sem("stored_odd")]

        sp_passed, pool_passed, dve_passed, pe_passed = (sem(f"{e}_passed") for e in ("sp", "pool", "dve", "pe"))

        n_consts = 7
        S_ALL, T_ALL = S_SUM[TILES], T_SUM[TILES]
        BIAS_PER = 3
        LOW = 6 * P
        block = ctx.enter_context(nc.Block())

        @block.sync
        def _(sp):
            for dst, src in ((ident, "ident"), (fold, "fold"), (cos, "cos"), (sin, "sin"),
                             (rel, "rel"), (mask, "mask"), (slopes, "slopes")):
                sp.dma_start(dst[:], ins[src]).then_inc(consts_loaded, 16)

            def load_piece(b, p, r):
                sp.dma_start(piece, ins["slabs"][3 * p + 2 + r, :, bass.ds(b * PIECE, PIECE)]) \
                    .then_inc(piece_loaded, 16)

            def load_w(pair):
                sp.dma_start(w_raw[:], ins["w_qkv"][pair]).then_inc(w_loaded, 16)
                sp.dma_start(b_raw[0:1, :], ins["b_qkv"][pair]).then_inc(w_loaded, 16)
                sp.dma_start(b_raw[32:33, :], ins["b_qkv"][pair]).then_inc(w_loaded, 16)

            sp.wait_ge(ones_ready, 1)
            load_w(0)
            with sp.Fori(0, B) as b:
                sp.dma_start(long_rows[:, :, :], ins["x_t"][b]).then_inc(x_loaded, 16)
                with sp.Fori(0, PAIRS) as p:
                    it = b * PAIRS + p
                    sp.wait_ge(w_split, it + 1)
                    load_piece(b, p, 0)
                    for q in range(GROUPS):
                        if q in (1, 3):
                            sp.wait_ge(piece_split, (it * PIECES + q // 2 + 1) * 2)
                            load_piece(b, p, q // 2 + 1)
                        if q == 5:
                            sp.wait_ge(piece_split, (it + 1) * PIECES * 2)
                            load_w(p + 1)
                        sp.wait_ge(normed, it * GROUPS + q + 1)
                        hold(sp, sp_passed)
                        first = TILE_OF[2 * q]
                        dst = attn_dram[b, first:first + 2, :, 2 * p + HEAD_OF[2 * q], :]
                        sp.dma_start(dst.rearrange("t p d -> p t d"), o_nat[:, q % 2, :, :]) \
                            .then_inc(stored[q % 2], 16)
                    sp.wait_ge(pt_turned, (it + 1) * T_ALL)
                    hold(sp, sp_passed)
            for par in range(2):
                sp.wait_ge(stored[par], 16 * (B * PAIRS * GROUPS // 2 + 1))
            sp.wait_ge(w_loaded, 48 * (B * PAIRS + 1))
            sp.wait_ge(piece_loaded, 16 * B * PAIRS * PIECES)

        @block.gpsimd
        def _(pool):
            pool.memset(b_raw[:], 0.0)
            pool.memset(b_st[:].bitcast(F32), 0.0)
            pool.memset(ones[:].bitcast(F32), 0.0)
            pool.drain()
            pool.memset(ones[0:1, :].bitcast(F32), 1.0)
            pool.drain()
            pool.memset(ones[32:33, :].bitcast(F32), 1.0).then_inc(ones_ready, 1)

            def split_w(lots):
                pool.wait_ge(w_loaded, lots * 48)
                hold(pool, pool_passed)
                pool.tensor_copy(w_hi[:], w_raw[:])
                pool.tensor_copy(b_hi[:], b_raw[:])
                pool.tensor_copy(b_st[0:1, :], b_raw[0:1, :]).then_inc(w_hi_ready, 1)
                pool.wait_ge(w_hi_ready, lots * 2 - 1)
                pool.tensor_tensor(w_lo[:], w_raw[:], w_hi[:].bitcast(F32), ALU.subtract).then_inc(w_hi_ready, 1)
                pool.wait_ge(w_hi_ready, lots * 2)
                pool.tensor_tensor(b_st[32:33, :], b_raw[32:33, :], b_hi[32:33, :].bitcast(F32),
                                   ALU.subtract).then_inc(w_split, 1)
                pool.wait_ge(w_split, lots)
                hold(pool, pool_passed)

            def split_piece(it, r):
                n = it * PIECES + r
                pool.wait_ge(piece_loaded, (n + 1) * 16)
                if r:
                    pool.wait_ge(piece_done, n)
                hold(pool, pool_passed)
                pool.tensor_copy(piece_hi, piece).then_inc(piece_split, 1)
                pool.wait_ge(piece_split, n * 2 + 1)
                pool.tensor_tensor(piece_lo, piece, piece_hi.bitcast(F32), ALU.subtract).then_inc(piece_split, 1)

            pool.wait_ge(ones_ready, 1)
            split_w(1)
            pool.wait_ge(consts_loaded, 16 * n_consts)
            with pool.Fori(0, B * PAIRS) as it:
                for t in range(NT):
                    pool.wait_ge(proj_copied, it * NT + t + 1)
                    if t >= 2:
                        pool.wait_ge(rope_add, it * NT + t - 1)
                    src = proj[:, t % 3, 0:QK_COLS].rearrange("p (h r d) -> p h r d", h=4, r=2)
                    cos_t = cos[:, t, :].rearrange("p (a b d) -> p a b d", a=1, b=1)
                    pool.tensor_tensor(by_cos[:, t % 2, :].rearrange("p (h r d) -> p h r d", h=4, r=2),
                                       src, cos_t.to_broadcast([P, 4, 2, HALF]), ALU.mult)
                    for r in range(2):
                        sin_t = sin[:, t, r * HALF:(r + 1) * HALF].rearrange("p (a d) -> p a d", a=1)
                        out = by_sin[:, t % 2, :].rearrange("p (h r d) -> p h r d", h=4, r=2)[:, :, r, :]
                        last = pool.tensor_tensor(out, src[:, :, 1 - r, :],
                                                  sin_t.to_broadcast([P, 4, HALF]), ALU.mult)
                    last.then_inc(rope_mul, 1)
                pool.wait_ge(proj_done, (it + 1) * NT)
                hold(pool, pool_passed)
                for q in range(GROUPS):
                    last_key = TILE_OF[2 * q] + 1
                    if q >= 2:
                        pool.wait_ge(pv_done, it * GROUPS + q - 1)
                        hold(pool, pool_passed)
                    hi, lo = pt_of(q)
                    pool.memset(hi[:, last_key, 0:P].bitcast(F32), 0.0)
                    pool.memset(lo[:, last_key, 0:P].bitcast(F32), 0.0).then_inc(pt_zeroed, 1)
                    if q in (1, 2, 4):
                        split_piece(it, q // 2)
                    if q == 7:
                        pool.wait_ge(piece_done, (it + 1) * PIECES)
                        split_w(it + 2)

        @block.scalar
        def _(act):
            act.wait_ge(consts_loaded, 16 * n_consts)

            def build_bias(it, head, lo, hi):
                act.activation(bias_t[:, lo:hi], rel[:, lo:hi], ACT.Copy,
                               scale=slopes[:, bass.ds(it * 2 + head, 1)]).then_inc(bias_built, 1)

            act.preload_act_table(ACT.Exp)
            with act.Fori(0, B * PAIRS, PAIRS) as b0:
                act.wait_ge(x_loaded, b0 * 2 + 16)
                act.activation(x_hi[:], long_rows[:, :, :], ACT.Copy).then_inc(x_hi_ready, PAIRS)
                with act.Fori(b0, b0 + PAIRS) as it:
                    for step in range(NT + 2):
                        t = step
                        if t < NT:
                            act.wait_ge(proj_done, it * NT + t + 1)
                            if t == 0:
                                act.wait_ge(x_lo_ready, b0 + PAIRS)
                            if t >= 3:
                                act.wait_ge(rope_mul, it * NT + t - 2)
                                act.wait_ge(v_lo_ready, it * NT + t - 2)
                            act.activation(proj[:, t % 3, :], ps_s[:, t % 3, 0:PAIR_COLS], ACT.Copy) \
                                .then_inc(proj_copied, 1)
                            act.wait_ge(proj_copied, it * NT + t + 1)
                            act.activation(v_st[:, :, t, 0:DH],
                                           proj[:, t % 3, QK_COLS:PAIR_COLS].rearrange("p (h d) -> p h d", h=2),
                                           ACT.Copy).then_inc(v_hi_ready, 1)
                            if t == 0:
                                build_bias(it, 0, 0, S)
                        t = step - 2
                        if t >= 0:
                            act.wait_ge(qk_turned, it * NT + t + 1)
                            turned = ps_t[:, t % 3, :].rearrange("p (h c) -> p h c", h=4)
                            act.activation(q_st[:, :, t * P:(t + 1) * P], turned[:, 0:2, :], ACT.Copy,
                                           scale=Q_SCALE)
                            act.activation(k_hi[:, :, t * P:(t + 1) * P], turned[:, 2:4, :], ACT.Copy) \
                                .then_inc(qk_hi_ready, 1)

                    def exp(j):
                        width = P * (TILE_OF[j] + 1)
                        act.wait_ge(biased, it * S_ALL + S_SUM[j + 1])
                        rows = rows_of(j)[:, 0:width]
                        n = len(s_chunks(j)) - 1
                        act.activation(rows, rows, ACT.Exp, bias=row_min[:, j, n:n + 1], scale=-1.0,
                                       accum_out=row_sum[:, j:j + 1]).then_inc(exped, 1)

                    def pt_high(j, c):
                        k0, n = t_chunks(j)[c]
                        i = T_SUM[j] + c
                        q = j // 2
                        if c == 0 and q >= 2:
                            act.wait_ge(pv_done, it * GROUPS + q - 1)
                        act.wait_ge(pt_turned, it * T_ALL + i + 1)
                        act.activation(pt_of(q)[0][:, k0:k0 + n, (j % 2) * P:(j % 2 + 1) * P],
                                       ps_t[:, i % 3, 0:n * P].rearrange("p (k c) -> p k c", k=n),
                                       ACT.Copy).then_inc(pt_hi_ready, 1)

                    for j in range(AHEAD - 1):
                        exp(j)
                    for j in range(TILES + 3):
                        if j >= 4 and j % 2 == 0:
                            q = (j - 4) // 2
                            act.wait_ge(pv_done, it * GROUPS + q + 1)
                            if q >= 2:
                                act.wait_ge(folded, it * GROUPS + q - 1)
                            act.activation(o_sb[:, q % 2, :], ps_v[:, q % 2, :], ACT.Copy).then_inc(o_copied, 1)
                        if j < TILES:
                            n = len(t_chunks(j))
                            for c in range(n):
                                pt_high(j, c)
                            if j + AHEAD - 1 < TILES:
                                exp(j + AHEAD - 1)
                            if j + AHEAD - 1 == 10:
                                act.wait_ge(biased, it * S_ALL + S_SUM[10])
                                build_bias(it, 1, 0, LOW)
                            if j + AHEAD - 1 == NT - 1:
                                build_bias(it, 1, LOW, S)

        @block.vector
        def _(dve):
            for par in range(2):
                dve.memset(o_nat[:, par, :, :], 0.0).then_inc(stored[par], 16)
            dve.wait_ge(consts_loaded, 16 * n_consts)
            with dve.Fori(0, B * PAIRS, PAIRS) as b0:
                dve.wait_ge(x_hi_ready, b0 + PAIRS)
                dve.tensor_tensor(x_lo[:], long_rows[:, :, :], x_hi[:].bitcast(F32), ALU.subtract) \
                    .then_inc(x_lo_ready, PAIRS)
                with dve.Fori(b0, b0 + PAIRS) as it:
                    def mask_bias(n):
                        dve.wait_ge(bias_built, it * BIAS_PER + n)
                        dve.tensor_tensor(bias_t[:, S - P:S], bias_t[:, S - P:S], mask[:], ALU.add) \
                            .then_inc(bias_masked, 1)

                    for step in range(NT + 2):
                        t = step - 1
                        if 0 <= t < NT:
                            dve.wait_ge(rope_mul, it * NT + t + 1)
                            if t >= 2:
                                dve.wait_ge(qk_turned, it * NT + t - 1)
                            shape = [P, 4, 2, DH]
                            dve.tensor_tensor(
                                roped[:, t % 2],
                                by_cos[:, t % 2, :].rearrange("p (h r d) -> p h r d", h=4, r=1).to_broadcast(shape),
                                by_sin[:, t % 2, :].rearrange("p (h r d) -> p h r d", h=4, r=1).to_broadcast(shape),
                                ALU.add).then_inc(rope_add, 1)
                            dve.wait_ge(v_hi_ready, it * NT + t + 1)
                            dve.tensor_tensor(v_st[:, :, t, DH:2 * DH],
                                              proj[:, t % 3, QK_COLS:PAIR_COLS].rearrange("p (h d) -> p h d", h=2),
                                              v_st[:, :, t, 0:DH].bitcast(F32), ALU.subtract).then_inc(v_lo_ready, 1)
                        t = step - 2
                        if t == 1:
                            mask_bias(1)
                        if t >= 0:
                            dve.wait_ge(qk_hi_ready, it * NT + t + 1)
                            turned = ps_t[:, t % 3, :].rearrange("p (h c) -> p h c", h=4)
                            cols = slice(t * P, (t + 1) * P)
                            dve.scalar_tensor_tensor(q_st[DH:P, :, cols], turned[DH:P, 0:2, :], Q_SCALE,
                                                     q_st[DH:P, :, cols].bitcast(F32), ALU.mult, ALU.subtract)
                            dve.tensor_tensor(k_lo[:, :, cols], turned[:, 2:4, :],
                                              k_hi[:, :, cols].bitcast(F32), ALU.subtract) \
                                .then_inc(qk_lo_ready, 1)

                    def add_bias(j, chunks):
                        if j == NT and 0 in chunks:
                            mask_bias(3)
                        for c, (k0, width) in enumerate(s_chunks(j)):
                            if c not in chunks:
                                continue
                            i = S_SUM[j] + c
                            if c == 0:
                                if j >= 4:
                                    dve.wait_ge(pt_turned, it * T_ALL + T_SUM[j - 3])
                                dve.wait_ge(bias_masked, it * 2 + HEAD_OF[j] + 1)
                            else:
                                dve.wait_ge(biased, it * S_ALL + i)
                            dve.wait_ge(scored, it * S_ALL + i + 1)
                            hold(dve, dve_passed)
                            off = S - P - P * TILE_OF[j] + k0
                            dve.tensor_tensor_reduce(
                                rows_of(j)[:, k0:k0 + width], ps_s[:, i % 3, 0:width], bias_t[:, off:off + width],
                                1.0, 3.0e38 if c == 0 else row_min[:, j, c - 1:c], ALU.add, ALU.min,
                                row_min[:, j, c:c + 1]).then_inc(biased, 1)

                    def pt_low(j, c):
                        k0, n = t_chunks(j)[c]
                        i = T_SUM[j] + c
                        hi, lo = pt_of(j // 2)
                        cols = slice((j % 2) * P, (j % 2 + 1) * P)
                        dve.wait_ge(pt_hi_ready, it * T_ALL + i + 1)
                        dve.tensor_tensor(lo[:, k0:k0 + n, cols],
                                          ps_t[:, i % 3, 0:n * P].rearrange("p (k c) -> p k c", k=n),
                                          hi[:, k0:k0 + n, cols].bitcast(F32), ALU.subtract) \
                            .then_inc(pt_lo_ready, 1)

                    dve.wait_ge(v_lo_ready, (it + 1) * NT)
                    for j in range(AHEAD):
                        add_bias(j, range(4))
                    def norm(q):
                        dve.wait_ge(exped, it * TILES + 2 * q + 2)
                        dve.reciprocal(row_inv[:, 2 * q:2 * q + 2], row_sum[:, 2 * q:2 * q + 2]) \
                            .then_inc(inverted, 1)
                        dve.wait_ge(folded, it * GROUPS + q + 1)
                        dve.wait_ge(stored[q % 2], (it * (GROUPS // 2) + q // 2 + 1) * 16)
                        dve.wait_ge(inverted, it * GROUPS + q + 1)
                        inv = row_inv[:, 2 * q:2 * q + 2].rearrange("p (t a) -> p t a", a=1)
                        dve.tensor_tensor(o_nat[:, q % 2, :, :],
                                          ps_n[:, q % 2, :].rearrange("p (t d) -> p t d", t=2),
                                          inv.to_broadcast([P, 2, DH]), ALU.mult).then_inc(normed, 1)

                    for j in range(TILES + 3):
                        n = len(t_chunks(j)) if j < TILES else 0
                        for r in range(4):
                            if r < n:
                                pt_low(j, r)
                            if j + AHEAD < TILES:
                                add_bias(j + AHEAD, range(r, r + 1))
                        if j >= 4 and j % 2 == 0:
                            norm((j - 4) // 2)
                        if j in (4, 8, 12):
                            n = it * PIECES + j // 4 - 1
                            dve.wait_ge(piece_split, n * 2 + 2)
                            hold(dve, dve_passed)
                            dve.tensor_reduce(lo_max[:, bass.ds(n, 1)], piece_lo.bitcast(F32),
                                              mybir.AxisListType.X, ALU.max,
                                              apply_absolute_value=True).then_inc(piece_done, 1)

        @block.tensor
        def _(pe):
            pe.wait_ge(consts_loaded, 16 * n_consts)
            pe.wait_ge(ones_ready, 1)
            with pe.Fori(0, B * PAIRS, PAIRS) as b0:
                pe.wait_ge(x_hi_ready, b0 + PAIRS)
                pe.wait_ge(x_lo_ready, b0 + PAIRS)
                hold(pe, pe_passed)
                with pe.Fori(b0, b0 + PAIRS) as it:
                    pe.wait_ge(w_split, it + 1)
                    for step in range(NT + 2):
                        t = step
                        if t < NT:
                            if t >= 3:
                                pe.wait_ge(proj_copied, it * NT + t - 2)
                            out = ps_s[:, t % 3, 0:PAIR_COLS]
                            rows = slice(t * P, (t + 1) * P)
                            pe.matmul(out, ones[:], b_st[:], start=True, stop=False)
                            for k in range(KD):
                                pe.matmul(out, x_hi[:, k, rows], w_hi[:, k, :], start=False, stop=False)
                                pe.matmul(out, x_hi[:, k, rows], w_lo[:, k, :], start=False, stop=False)
                                last = pe.matmul(out, x_lo[:, k, rows], w_hi[:, k, :], start=False,
                                                 stop=k == KD - 1)
                            last.then_inc(proj_done, 1)
                        t = step - 2
                        if t >= 0:
                            pe.wait_ge(rope_add, it * NT + t + 1)
                            if t >= 3:
                                pe.wait_ge(qk_lo_ready, it * NT + t - 2)
                            for h in range(4):
                                src = roped[:, t % 2, h].rearrange("p r d -> p (r d)")
                                last = pe.transpose(ps_t[:, t % 3, h * P:(h + 1) * P], src, ident[:])
                            last.then_inc(qk_turned, 1)

                    def score(j, chunks):
                        head, rows = HEAD_OF[j], slice(TILE_OF[j] * P, (TILE_OF[j] + 1) * P)
                        for c, (k0, width) in enumerate(s_chunks(j)):
                            if c not in chunks:
                                continue
                            i = S_SUM[j] + c
                            if i >= 3:
                                pe.wait_ge(biased, it * S_ALL + i - 2)
                            n = max(2 * P, width)
                            out = ps_s[:, i % 3, 0:n]
                            pe.matmul(out, q_st[:, head, rows], k_hi[:, head, k0:k0 + n], start=True, stop=False)
                            pe.matmul(out, q_st[:, head, rows], k_lo[:, head, k0:k0 + n],
                                      start=False, stop=True).then_inc(scored, 1)

                    def turn(j, c):
                        k0, n = t_chunks(j)[c]
                        i = T_SUM[j] + c
                        if i >= 3:
                            pe.wait_ge(pt_lo_ready, it * T_ALL + i - 2)
                        if c == 0:
                            pe.wait_ge(exped, it * TILES + j + 1)
                        for k in range(n):
                            last = pe.transpose(ps_t[:, i % 3, k * P:(k + 1) * P],
                                                rows_of(j)[:, (k0 + k) * P:(k0 + k + 1) * P], ident[:])
                        last.then_inc(pt_turned, 1)

                    def weigh(q, half, quarter):
                        keys = TILE_OF[2 * q] + 2
                        head = HEAD_OF[2 * q]
                        hi, lo = pt_of(q)
                        if half == 0 and quarter == 0:
                            pe.wait_ge(pt_lo_ready, it * T_ALL + T_SUM[2 * q + 2])
                            pe.wait_ge(pt_zeroed, it * GROUPS + q + 1)
                            if q >= 2:
                                pe.wait_ge(normed, it * GROUPS + q - 1)
                        first = half * keys // 2
                        for k in range(first + quarter * keys // 8, first + (quarter + 1) * keys // 8):
                            for part in (hi, lo):
                                last = pe.matmul(ps_v[:, q % 2, :], v_st[:, head, k, :], part[:, k, :],
                                                 start=k == 0 and part is hi, stop=k == keys - 1 and part is lo)
                                if k == keys - 1 and part is lo:
                                    last.then_inc(pv_done, 1)

                    def add_parts(q):
                        pe.wait_ge(o_copied, it * GROUPS + q + 1)
                        for r in range(2):
                            last = pe.matmul(ps_n[:, q % 2, r * DH:(r + 1) * DH], o_sb[:, q % 2, r * P:(r + 1) * P],
                                             fold[:], start=True, stop=True)
                        last.then_inc(folded, 1)

                    pe.wait_ge(proj_copied, (it + 1) * NT)
                    pe.wait_ge(v_lo_ready, (it + 1) * NT)
                    pe.wait_ge(qk_lo_ready, (it + 1) * NT)
                    for j in range(AHEAD):
                        score(j, range(4))
                    for j in range(TILES + 3):
                        n = len(t_chunks(j)) if j < TILES else 0
                        for r in range(4):
                            if r < n:
                                turn(j, r)
                            if r == 1 and j >= 4 and j % 2 == 0:
                                add_parts((j - 4) // 2)
                            if j + AHEAD < TILES:
                                score(j + AHEAD, range(r, r + 1))
                        if 2 <= j < TILES + 2:
                            for r in range(4):
                                weigh((j - 2) // 2, j % 2, r)
                    pe.wait_ge(biased, (it + 1) * S_ALL)
                    pe.wait_ge(pt_lo_ready, (it + 1) * T_ALL)
                    pe.wait_ge(normed, (it + 1) * GROUPS)
                    hold(pe, pe_passed)


SLABS = 2 + MT // 2 + 2 * MT + 2
SLAB = 1024
SLAB_UP, SLAB_HID, SLAB_DOWN = 2, 2 + MT // 2, 2 + MT // 2 + 2 * MT
HALVES = TOK // BANK


def feed_forward(nc, ins, attn_dram, lo_max, out):
    ctx = ExitStack()
    with ctx:
        def sb(name, shape, dt=F32):
            return ctx.enter_context(nc.sbuf_tensor(name, shape, dt))

        def sem(name):
            return ctx.enter_context(nc.semaphore(name))

        slab_raw = sb("slab_raw", [P, 2, SLAB])
        slab_hi = sb("slab_hi", [P, 2, SLAB], F32R)
        slab_lo = sb("slab_lo", [P, 2, SLAB], F32R)
        attn = sb("attn", [P, 2, H * DH])
        y_nat = sb("y_nat", [P, TT, DM])
        y_hi = sb("y_hi", [P, KD, TOK], F32R)
        y_lo = sb("y_lo", [P, KD, TOK], F32R)
        ha_hi = sb("ha_hi", [P, MT, TOK], F32R)
        ha_lo = sb("ha_lo", [P, MT, TOK], F32R)
        hb_hi = sb("hb_hi", [P, MT, TOK], F32R)
        hb_lo = sb("hb_lo", [P, MT, TOK], F32R)
        silu = sb("silu", [P, 2, BANK])
        hid = sb("hid", [P, 2, BANK])
        ident = sb("ident_f", [P, P])
        s_hid = sb("s_hid", [P, 4, MT])
        b_out = sb("b_out", [P, DM])
        s_down = sb("s_down", [P, DM])
        eps = sb("eps", [P, 1])
        stats = sb("stats", [P, TT, 6])
        moments = sb("moments", [P, TT, 2])
        std = sb("std", [P, TT])
        rstd = sb("rstd", [P, TT])
        largest_lo = sb("largest_lo", [P, 1])
        has_lo = sb("has_lo", [P, 1])
        ones = sb("ones_f", [P, 1])
        rows_with_lo = sb("rows_with_lo", [1, 1], mybir.dt.int32)

        ps_m = ctx.enter_context(nc.psum_tensor("ps_m", [P, 4, BANK], F32))
        ps_acc = ctx.enter_context(nc.psum_tensor("ps_acc", [P, TT, DM], F32))

        consts_loaded = sem("f_consts_loaded")
        eps_ready = sem("eps_ready")
        raw_loaded = [sem("raw_loaded_even"), sem("raw_loaded_odd")]
        slab_hi_ready = sem("slab_hi_ready")
        slab_ready = sem("slab_ready")
        slab_used = sem("slab_used")
        x_loaded = sem("f_x_loaded")
        attn_loaded = [sem("attn_loaded_even"), sem("attn_loaded_odd")]
        x_biased = sem("x_biased")
        attn_turned = sem("attn_turned")
        attn_hi_ready = sem("attn_hi_ready")
        attn_lo_ready = sem("attn_lo_ready")
        acc_done = sem("acc_done")
        step_done = sem("step_done")
        var_ready = sem("var_ready")
        std_ready = sem("std_ready")
        y_ready = sem("y_ready")
        y_turned = sem("y_turned")
        y_hi_ready = sem("y_hi_ready")
        y_lo_ready = sem("y_lo_ready")
        up_done = sem("up_done")
        silu_ready = sem("silu_ready")
        gated = sem("gated")
        up_hi_ready = sem("up_hi_ready")
        up_lo_ready = sem("up_lo_ready")
        hid_done = sem("hid_done")
        gelu_ready = sem("gelu_ready")
        hid_hi_ready = sem("hid_hi_ready")
        hid_lo_ready = sem("hid_lo_ready")
        out_ready = sem("out_ready")
        out_stored = sem("out_stored")
        flag_step = sem("flag_step")

        sp_passed, pool_passed, dve_passed, pe_passed = (sem(f"f_{e}_passed") for e in ("sp", "pool", "dve", "pe"))

        tokens = "(c t p) d -> c p t d"
        x_rows = ins["x"].rearrange("b s d -> (b s) d").rearrange(tokens, t=TT, p=P)
        out_rows = out.rearrange("b s d -> (b s) d").rearrange(tokens, t=TT, p=P)
        attn_rows = attn_dram.rearrange("b t p h d -> (b t) p (h d)").rearrange("(c t) p d -> c t p d", t=TT)
        UP_UNITS = MT * HALVES
        HID_UNITS = 2 * MT * HALVES
        CHAIN = 3 * TT + 2 * (TT + 1)
        n_consts = 4

        def hid_place(n):
            return n // UP_UNITS, n % UP_UNITS // HALVES, slice(n % HALVES * BANK, (n % HALVES + 1) * BANK)

        block = ctx.enter_context(nc.Block())

        @block.sync
        def _(sp):
            sp.dma_start(ident[:], ins["ident"]).then_inc(consts_loaded, 16)
            sp.dma_start(s_hid[:], ins["s_hid"]).then_inc(consts_loaded, 16)
            sp.dma_start(b_out[:], ins["b_out"].to_broadcast([P, DM])).then_inc(consts_loaded, 16)
            sp.dma_start(s_down[:], ins["s_down"].to_broadcast([P, DM])).then_inc(consts_loaded, 16)
            for s in range(2):
                sp.dma_start(slab_raw[:, s, :], ins["slabs"][s]).then_inc(raw_loaded[s], 16)
            with sp.Fori(0, CHUNKS) as c:
                sp.dma_start(y_nat[:], x_rows[c]).then_inc(x_loaded, 16)
                for s in range(SLABS):
                    sp.wait_ge(slab_ready, c * SLABS + s + 1)
                    sp.dma_start(slab_raw[:, s % 2, :], ins["slabs"][(s + 2) % SLABS]) \
                        .then_inc(raw_loaded[s % 2], 16)
                sp.wait_ge(out_ready, c * TT + TT)
                sp.dma_start(out_rows[c], y_nat[:]).then_inc(out_stored, 16)
                sp.wait_ge(out_stored, c * 16 + 16)
                hold(sp, sp_passed)
            sp.wait_ge(out_stored, CHUNKS * 16)
            for par in range(2):
                sp.wait_ge(raw_loaded[par], 16 * (CHUNKS * SLABS // 2 + 1))

        @block.gpsimd
        def _(pool):
            pool.memset(eps[:], EPS).then_inc(eps_ready, 1)

            def split(s, loads, lots):
                pool.wait_ge(raw_loaded[s % 2], loads * 16)
                hold(pool, pool_passed)
                pool.tensor_copy(slab_hi[:, s % 2, :], slab_raw[:, s % 2, :]).then_inc(slab_hi_ready, 1)
                pool.wait_ge(slab_hi_ready, lots)
                pool.tensor_tensor(slab_lo[:, s % 2, :], slab_raw[:, s % 2, :],
                                   slab_hi[:, s % 2, :].bitcast(F32), ALU.subtract).then_inc(slab_ready, 1)

            split(0, 1, 1)
            split(1, 1, 2)
            pool.wait_ge(consts_loaded, 16 * n_consts)
            with pool.Fori(0, CHUNKS) as c:
                pool.wait_ge(x_loaded, c * 16 + 16)
                for t in range(TT):
                    last = pool.tensor_tensor(y_nat[:, t, :], y_nat[:, t, :], b_out[:], ALU.add)
                    last.then_inc(x_biased, 1)
                for s in range(SLABS):
                    pool.wait_ge(slab_used, c * SLABS + s + 1)
                    split(s, c * (SLABS // 2) + s // 2 + 2, c * SLABS + s + 3)

        @block.scalar
        def _(act):
            def load_attn(c, t):
                act.dma_start(attn[:, t % 2, :], attn_rows[c, t]).then_inc(attn_loaded[t % 2], 16)

            act.wait_ge(eps_ready, 1)
            act.wait_ge(consts_loaded, 16 * n_consts)
            with act.Fori(0, CHUNKS) as c:
                load_attn(c, 0)
                load_attn(c, 1)
                for u in range(2 * TT):
                    t, k0 = u // 2, u % 2 * 4
                    act.wait_ge(attn_turned, c * 2 * TT + u + 1)
                    act.activation(hb_hi[:, k0:k0 + 4, t * P:(t + 1) * P],
                                   ps_m[:, u % 4, :].rearrange("p (k c) -> p k c", k=4), ACT.Copy) \
                        .then_inc(attn_hi_ready, 1)
                    if u % 2 and t + 2 < TT:
                        load_attn(c, t + 2)

                def sqrt(n):
                    act.wait_ge(var_ready, (c * 2 + n) * TT)
                    act.activation(std[:], moments[:, :, 1], ACT.Sqrt, bias=eps[:]).then_inc(std_ready, 1)

                sqrt(1)
                for u in range(TT // 2):
                    act.wait_ge(y_turned, c * (TT // 2) + u + 1)
                    act.activation(y_hi[:, :, u * 2 * P:(u + 1) * 2 * P].rearrange("p k (t c) -> p t k c", t=2),
                                   ps_m[:, u % 4, :].rearrange("p (t k c) -> p t k c", t=2, k=KD), ACT.Copy) \
                        .then_inc(y_hi_ready, 1)
                for n in range(UP_UNITS + 1):
                    if n < UP_UNITS:
                        act.wait_ge(up_done, c * UP_UNITS + n + 1)
                        if n >= 2:
                            act.wait_ge(gated, c * UP_UNITS + n - 1)
                        act.activation(silu[:, n % 2, :], ps_m[:, n % 2 * 2, :], ACT.Silu,
                                       scale=s_hid[:, 0, n // HALVES:n // HALVES + 1]).then_inc(silu_ready, 1)
                    if n >= 1:
                        m, cols = (n - 1) // HALVES, slice((n - 1) % HALVES * BANK, ((n - 1) % HALVES + 1) * BANK)
                        act.wait_ge(gated, c * UP_UNITS + n)
                        act.activation(ha_hi[:, m, cols], hid[:, (n - 1) % 2, :], ACT.Copy).then_inc(up_hi_ready, 1)
                for n in range(HID_UNITS):
                    layer, m, cols = hid_place(n)
                    act.wait_ge(hid_done, c * HID_UNITS + n + 1)
                    if n >= 2:
                        act.wait_ge(hid_lo_ready, c * HID_UNITS + n - 1)
                    act.activation(hid[:, n % 2, :], ps_m[:, n % 4, :], ACT.Gelu,
                                   scale=s_hid[:, 2 + layer, m:m + 1]).then_inc(gelu_ready, 1)
                    act.wait_ge(gelu_ready, c * HID_UNITS + n + 1)
                    act.activation((ha_hi if layer else hb_hi)[:, m, cols], hid[:, n % 2, :], ACT.Copy) \
                        .then_inc(hid_hi_ready, 1)
                sqrt(2)

        @block.vector
        def _(dve):
            dve.memset(ones[:], 1.0)
            dve.tensor_reduce(largest_lo[:], lo_max[:, 0:B * PAIRS * PIECES], mybir.AxisListType.X,
                              ALU.max,
                                              apply_absolute_value=True).then_inc(flag_step, 1)
            dve.wait_ge(flag_step, 1)
            dve.tensor_scalar(has_lo[:], largest_lo[:], 0.0, None, ALU.is_gt).then_inc(flag_step, 1)
            dve.wait_ge(flag_step, 3)
            dve.tensor_copy(rows_with_lo[:], ps_m[0:1, 0, 0:1]).then_inc(flag_step, 1)
            dve.wait_ge(consts_loaded, 16 * n_consts)
            with dve.Fori(0, CHUNKS) as c:
                for u in range(2 * TT):
                    t, k0 = u // 2, u % 2 * 4
                    dve.wait_ge(attn_hi_ready, c * 2 * TT + u + 1)
                    dve.tensor_tensor(hb_lo[:, k0:k0 + 4, t * P:(t + 1) * P],
                                      ps_m[:, u % 4, :].rearrange("p (k c) -> p k c", k=4),
                                      hb_hi[:, k0:k0 + 4, t * P:(t + 1) * P].bitcast(F32), ALU.subtract) \
                        .then_inc(attn_lo_ready, 1)

                steps = [0]

                def chained(op):
                    steps[0] += 1
                    op.then_inc(step_done, 1)

                def wait_chain(back=0):
                    dve.wait_ge(step_done, c * CHAIN + steps[0] - back)

                def layernorm(n, ready):
                    for t in range(TT):
                        chained(dve.bn_stats(stats[:, t, :], y_nat[:, t, :]))
                    for t in range(TT):
                        wait_chain(TT - 1 - t)
                        hold(dve, dve_passed)
                        dve.bn_aggr(moments[:, t, :], stats[:, t, :]).then_inc(var_ready, 1)
                    dve.wait_ge(std_ready, c * 2 + n)
                    chained(dve.reciprocal(rstd[:], std[:]))
                    wait_chain()
                    for t in range(TT):
                        dve.tensor_scalar(y_nat[:, t, :], y_nat[:, t, :], moments[:, t, 0:1], rstd[:, t:t + 1],
                                          ALU.subtract, ALU.mult).then_inc(ready, 1)

                for t in range(TT):
                    dve.wait_ge(x_biased, c * TT + t + 1)
                    dve.wait_ge(acc_done, c * 2 * TT + (t | 1) + 1)
                    chained(dve.tensor_tensor(y_nat[:, t, :], ps_acc[:, t, :], y_nat[:, t, :], ALU.add))
                wait_chain()
                layernorm(1, y_ready)
                for u in range(TT // 2):
                    dve.wait_ge(y_hi_ready, c * (TT // 2) + u + 1)
                    view = lambda a: a[:, :, u * 2 * P:(u + 1) * 2 * P].rearrange("p k (t c) -> p t k c", t=2)
                    dve.tensor_tensor(view(y_lo), ps_m[:, u % 4, :].rearrange("p (t k c) -> p t k c", t=2, k=KD),
                                      view(y_hi).bitcast(F32), ALU.subtract).then_inc(y_lo_ready, 1)
                for n in range(UP_UNITS + 1):
                    if n < UP_UNITS:
                        m = n // HALVES
                        if n >= 2:
                            dve.wait_ge(up_lo_ready, c * UP_UNITS + n - 1)
                        dve.wait_ge(silu_ready, c * UP_UNITS + n + 1)
                        dve.scalar_tensor_tensor(hid[:, n % 2, :], ps_m[:, n % 2 * 2 + 1, :], s_hid[:, 1, m:m + 1],
                                                 silu[:, n % 2, :], ALU.mult, ALU.mult).then_inc(gated, 1)
                    if n >= 1:
                        m, cols = (n - 1) // HALVES, slice((n - 1) % HALVES * BANK, ((n - 1) % HALVES + 1) * BANK)
                        dve.wait_ge(up_hi_ready, c * UP_UNITS + n)
                        dve.tensor_tensor(ha_lo[:, m, cols], hid[:, (n - 1) % 2, :], ha_hi[:, m, cols].bitcast(F32),
                                          ALU.subtract).then_inc(up_lo_ready, 1)
                for n in range(HID_UNITS):
                    layer, m, cols = hid_place(n)
                    dve.wait_ge(hid_hi_ready, c * HID_UNITS + n + 1)
                    dve.tensor_tensor((ha_lo if layer else hb_lo)[:, m, cols], hid[:, n % 2, :],
                                      (ha_hi if layer else hb_hi)[:, m, cols].bitcast(F32),
                                      ALU.subtract).then_inc(hid_lo_ready, 1)
                for t in range(TT):
                    dve.wait_ge(acc_done, c * 2 * TT + TT + (t | 1) + 1)
                    chained(dve.tensor_tensor(silu[:, t % 2, 0:DM], ps_acc[:, t, :], s_down[:], ALU.mult))
                    wait_chain()
                    chained(dve.tensor_tensor(y_nat[:, t, :], silu[:, t % 2, 0:DM], y_nat[:, t, :], ALU.add))
                wait_chain()
                layernorm(2, out_ready)
                assert steps[0] == CHAIN, steps[0]

        @block.tensor
        def _(pe):
            def chunk(c, lo_weights):
                for u in range(2 * TT):
                    t, k0 = u // 2, u % 2 * 4
                    if u % 2 == 0:
                        pe.wait_ge(attn_loaded[t % 2], (c * (TT // 2) + t // 2 + 1) * 16)
                    if u >= 4:
                        pe.wait_ge(attn_lo_ready, c * 2 * TT + u - 3)
                    for k in range(4):
                        last = pe.transpose(ps_m[:, u % 4, k * P:(k + 1) * P],
                                            attn[:, t % 2, (k0 + k) * P:(k0 + k + 1) * P], ident[:])
                    last.then_inc(attn_turned, 1)

                def rows_out(first, hi, lo):
                    for half in range(2):
                        s = first + half
                        pe.wait_ge(slab_ready, c * SLABS + s + 1)
                        for t in range(TT):
                            for kk in range(4):
                                k = half * 4 + kk
                                wh = slab_hi[:, s % 2, kk * DM:(kk + 1) * DM]
                                wl = slab_lo[:, s % 2, kk * DM:(kk + 1) * DM]
                                rows = slice(t * P, (t + 1) * P)
                                pe.matmul(ps_acc[:, t, :], hi[:, k, rows], wh, start=k == 0 and t % 2 == 0,
                                          stop=False, skip_group_check=True)
                                if first < SLAB_UP or lo_weights:
                                    pe.matmul(ps_acc[:, t, :], hi[:, k, rows], wl, start=False, stop=False,
                                              skip_group_check=True)
                                last = pe.matmul(ps_acc[:, t, :], lo[:, k, rows], wh, start=False,
                                                 stop=k == MT - 1, skip_group_check=True)
                            if half:
                                last.then_inc(acc_done, 1)
                        pe.drain().then_inc(slab_used, 1)

                pe.wait_ge(attn_lo_ready, (c + 1) * 2 * TT)
                rows_out(0, hb_hi, hb_lo)
                for u in range(TT // 2):
                    pe.wait_ge(y_ready, c * TT + 2 * u + 2)
                    for t in range(2):
                        for k in range(KD):
                            last = pe.transpose(ps_m[:, u % 4, (t * KD + k) * P:(t * KD + k + 1) * P],
                                                y_nat[:, 2 * u + t, k * P:(k + 1) * P], ident[:])
                    last.then_inc(y_turned, 1)
                pe.wait_ge(y_lo_ready, (c + 1) * (TT // 2))

                def product(out, s, at, hi, lo, cols, tiles):
                    for k in range(tiles):
                        wh = slab_hi[:, s % 2, at + k * P:at + (k + 1) * P]
                        wl = slab_lo[:, s % 2, at + k * P:at + (k + 1) * P]
                        pe.matmul(out, wh, hi[:, k, cols], start=k == 0, stop=False)
                        last = pe.matmul(out, wh, lo[:, k, cols], start=False,
                                         stop=k == tiles - 1 and not lo_weights)
                        if lo_weights:
                            last = pe.matmul(out, wl, hi[:, k, cols], start=False, stop=k == tiles - 1)
                    return last

                for n in range(UP_UNITS):
                    m, cols = n // HALVES, slice(n % HALVES * BANK, (n % HALVES + 1) * BANK)
                    s = SLAB_UP + m // 2
                    if n % (2 * HALVES) == 0:
                        pe.wait_ge(slab_ready, c * SLABS + s + 1)
                    if n >= 2:
                        pe.wait_ge(gated, c * UP_UNITS + n - 1)
                    for w in range(2):
                        last = product(ps_m[:, n % 2 * 2 + w, :], s, (m % 2 * 2 + w) * KD * P, y_hi, y_lo, cols, KD)
                    last.then_inc(up_done, 1)
                    if n % (2 * HALVES) == 2 * HALVES - 1:
                        pe.drain().then_inc(slab_used, 1)
                pe.wait_ge(up_lo_ready, (c + 1) * UP_UNITS)
                for n in range(HID_UNITS):
                    layer, m, cols = hid_place(n)
                    s = SLAB_HID + layer * MT + m
                    if n % HALVES == 0:
                        pe.wait_ge(slab_ready, c * SLABS + s + 1)
                    if n == UP_UNITS:
                        pe.wait_ge(hid_lo_ready, c * HID_UNITS + UP_UNITS)
                    elif n >= 4:
                        pe.wait_ge(gelu_ready, c * HID_UNITS + n - 3)
                    hi, lo = (hb_hi, hb_lo) if layer else (ha_hi, ha_lo)
                    product(ps_m[:, n % 4, :], s, 0, hi, lo, cols, MT).then_inc(hid_done, 1)
                    if n % HALVES == HALVES - 1:
                        pe.drain().then_inc(slab_used, 1)
                pe.wait_ge(hid_lo_ready, (c + 1) * HID_UNITS)
                rows_out(SLAB_DOWN, ha_hi, ha_lo)
                pe.wait_ge(out_ready, (c + 1) * TT)
                hold(pe, pe_passed)

            pe.wait_ge(flag_step, 2)
            pe.matmul(ps_m[0:1, 0, 0:1], has_lo[:], ones[:], start=True, stop=True).then_inc(flag_step, 1)
            pe.wait_ge(consts_loaded, 16 * n_consts)
            pe.wait_ge(flag_step, 4)
            with_lo = pe.value_load(rows_with_lo[0:1, 0:1])
            with pe.If(with_lo > 0):
                with pe.Fori(0, CHUNKS) as c:
                    chunk(c, True)
            with pe.If(with_lo < 1):
                with pe.Fori(0, CHUNKS) as c:
                    chunk(c, False)


def program(nc, ins, out):
    attn_dram = nc.dram_tensor("attn_scratch", (B, NT, P, H, DH), F32, kind="Internal").ap()
    with nc.sbuf_tensor("lo_max", [P, (B * PAIRS + PAIRS) * PIECES], F32) as lo_max:
        attention(nc, ins, attn_dram, lo_max)
        feed_forward(nc, ins, attn_dram, lo_max, out)


def _constants():
    import numpy as np

    pos = np.arange(S, dtype=np.float32)
    inv_freq = (1.0 / np.float32(10000.0) ** (np.arange(0, DH, 2, dtype=np.float32) / np.float32(DH))).astype(np.float32)
    freqs = np.outer(pos, inv_freq).astype(np.float32)
    rows = lambda a: np.ascontiguousarray(a.reshape(NT, P, -1).transpose(1, 0, 2)).astype(np.float32)
    start = 2.0 ** (-8.0 / H)
    slope = np.array([start ** (h + 1) for h in range(H)], np.float32) * np.float32(8.0)
    slopes = np.zeros(48, np.float32)
    slopes[0:2 * H] = np.tile(slope, 2)
    dist = np.arange(P)[:, None] - (np.arange(S)[None, :] - (S - P))
    return {
        "ident": np.eye(P, dtype=np.float32),
        "fold": np.concatenate([np.eye(DH, dtype=np.float32)] * 2),
        "cos": rows(np.cos(freqs)),
        "sin": rows(np.concatenate([-np.sin(freqs), np.sin(freqs)], axis=1)),
        "rel": np.maximum(dist, 0).astype(np.float16),
        "mask": np.where(dist[:, S - P:] < 0, np.float32(NEG_MASK), np.float32(0)).astype(np.float32),
        "slopes": np.ascontiguousarray(np.broadcast_to(slopes, (P, 48))),
    }


def kernel(L0_attn_x, L0_attn_w_qkv, L0_attn_b_qkv, L0_attn_w_out, L0_attn_b_out, L0_ffn_w1_w, L0_ffn_w1_s,
           L0_ffn_w2_w, L0_ffn_w2_s, L0_ffn_h1_w, L0_ffn_h1_s, L0_ffn_h2_w, L0_ffn_h2_s, L0_ffn_w3_w, L0_ffn_w3_s):
    import numpy as np
    import concourse.bacc as bacc
    from concourse.bass_utils import run_bass_kernel_spmd

    c = np.ascontiguousarray
    a = lambda v: np.asarray(v)

    def by_pair(w):
        w = w.reshape(w.shape[0], PAIRS, 2, 3, DH).transpose(1, 0, 3, 2, 4).reshape(PAIRS, w.shape[0], PAIR_COLS)
        return np.concatenate([w, w[0:1]])

    w_qkv = by_pair(a(L0_attn_w_qkv)).reshape(PAIRS + 1, KD, P, PAIR_COLS).transpose(0, 2, 1, 3)
    rows_k = lambda w: w.reshape(2, 4, P, DM).transpose(0, 2, 1, 3).reshape(2, P, SLAB)
    cols_m = lambda w: w.reshape(MT, P, -1, P).transpose(0, 3, 2, 1)
    up = np.stack([cols_m(a(L0_ffn_w1_w)), cols_m(a(L0_ffn_w2_w))], axis=2)
    up = up.reshape(MT // 2, 2, P, 2, KD, P).transpose(0, 2, 1, 3, 4, 5).reshape(MT // 2, P, SLAB)
    slabs = np.concatenate([
        rows_k(a(L0_attn_w_out).reshape(H * DH, DM)), up,
        cols_m(a(L0_ffn_h1_w)).reshape(MT, P, SLAB), cols_m(a(L0_ffn_h2_w)).reshape(MT, P, SLAB),
        rows_k(a(L0_ffn_w3_w).T),
    ])
    slabs = np.concatenate([slabs, slabs[-2:]])
    scales = np.stack([a(s).reshape(MT, P) for s in (L0_ffn_w1_s, L0_ffn_w2_s, L0_ffn_h1_s, L0_ffn_h2_s)])
    arrays = _constants() | {
        "x": a(L0_attn_x),
        "x_t": a(L0_attn_x).transpose(0, 2, 1).reshape(B, KD, P, S).transpose(0, 2, 1, 3),
        "w_qkv": w_qkv,
        "b_qkv": by_pair(a(L0_attn_b_qkv).reshape(1, H * 3 * DH)),
        "slabs": slabs,
        "s_hid": scales.transpose(2, 0, 1),
        "b_out": a(L0_attn_b_out).reshape(1, DM),
        "s_down": a(L0_ffn_w3_s).reshape(1, DM),
    }
    nc = bacc.Bacc("TRN2", target_bir_lowering=False, num_devices=1)
    feed, ins = {}, {}
    for name, v in arrays.items():
        feed[f"in_{name}"] = c(v)
        ins[name] = nc.dram_tensor(f"in_{name}", v.shape, mybir.dt.from_np(v.dtype), kind="ExternalInput").ap()
    out = nc.dram_tensor("out_rows", (B, S, DM), F32, kind="ExternalOutput").ap()
    program(nc, ins, out)
    return run_bass_kernel_spmd(nc, [feed], core_ids=[0]).results[0]["out_rows"]
```

```python
from contextlib import ExitStack

import concourse.bass as bass
from concourse import mybir

F32 = mybir.dt.float32
F32R = mybir.dt.float32r
F16 = mybir.dt.float16
I32 = mybir.dt.int32
ALU = mybir.AluOpType
ACT = mybir.ActivationFunctionType

P = 128
B, S, DM, H, DH = 2, 2048, 256, 16, 64
KD = DM // P
NT = S // P
PAIRS = H // 2
PAIR_COLS = 2 * 3 * DH
QK_COLS = 2 * 2 * DH
HALF = DH // 2
Q_SCALE = -1.0 / float(3 * DH) ** 0.5
BANK = 512
NEG_MASK = 1.0e12

ORDER = [t for g in range(NT // 4) for t in (2 * g, 2 * g + 1, NT - 2 - 2 * g, NT - 1 - 2 * g)]
AHEAD = 3
TILES = 2 * NT
GROUPS = TILES // 2
HEAD_OF = [j // NT for j in range(TILES)]
TILE_OF = [ORDER[j % NT] for j in range(TILES)]

D_HID = 1024
MT = D_HID // P
TOK = 1024
CHUNKS = B * S // TOK
TT = TOK // P
EPS = 1e-5


NX = 4
XC = S // NX
PIECE = 512
PIECES = 3


def hold(eng, passed):
    eng.sem_inc(passed, 1)


def s_chunks(j):
    width = P * (TILE_OF[j] + 1)
    return [(c, min(BANK, width - c)) for c in range(0, width, BANK)]


def bank(i):
    return (NT + i) % 3


def t_chunks(j):
    n = TILE_OF[j] + 1
    return [(k, min(4, n - k)) for k in range(0, n, 4)]


S_SUM = [sum(len(s_chunks(i)) for i in range(j)) for j in range(TILES + 1)]
T_SUM = [sum(len(t_chunks(i)) for i in range(j)) for j in range(TILES + 1)]


def attention(nc, ins, attn_dram, lo_max):
    ctx = ExitStack()
    with ctx:
        def sb(name, shape, dt=F32):
            return ctx.enter_context(nc.sbuf_tensor(name, shape, dt))

        def sem(name):
            return ctx.enter_context(nc.semaphore(name))

        x_hi = sb("x_hi", [P, KD, S], F32R)
        x_lo = sb("x_lo", [P, KD, S], F32R)
        rel = sb("rel", [P, S], F16)
        mask = sb("mask", [P, P])
        bias_t = sb("bias_t", [P, S])
        k_hi = sb("k_hi", [P, 2, S], F32R)
        k_lo = sb("k_lo", [P, 2, S], F32R)
        q_st = sb("q_st", [P, 2, S], F32R)
        v_st = sb("v_st", [P, 2, NT, 2 * DH], F32R)
        long_rows = sb("long_rows", [P, 2, S])
        short_rows = sb("short_rows", [P, 2, S // 2])
        pt_long_hi = sb("pt_long_hi", [P, NT, 2 * P], F32R)
        pt_long_lo = sb("pt_long_lo", [P, NT, 2 * P], F32R)
        pt_short_hi = sb("pt_short_hi", [P, NT // 2, 2 * P], F32R)
        pt_short_lo = sb("pt_short_lo", [P, NT // 2, 2 * P], F32R)
        o_sb = sb("o_sb", [P, 2, 2 * P])
        o_nat = sb("o_nat", [P, 2, 2, DH])
        cos = sb("cos", [P, NT, HALF])
        sin = sb("sin", [P, NT, DH])
        w_raw = sb("w_raw", [P, KD, PAIR_COLS])
        w_hi = sb("w_hi", [P, KD, PAIR_COLS], F32R)
        w_lo = sb("w_lo", [P, KD, PAIR_COLS], F32R)
        b_raw = sb("b_raw", [DH, PAIR_COLS])
        b_hi = sb("b_hi", [DH, PAIR_COLS], F32R)
        b_st = sb("b_st", [P, PAIR_COLS], F32R)
        ones = sb("ones", [P, P], F32R)
        ident = sb("ident", [P, P])
        fold = sb("fold", [P, DH])
        slopes = sb("slopes", [P, 48])
        row_min = sb("row_min", [P, TILES, 4])
        row_sum = sb("row_sum", [P, TILES])
        row_inv = sb("row_inv", [P, TILES])

        piece, piece_hi, piece_lo = (w[:, :, :].rearrange("p k c -> p (k c)")[:, 0:PIECE]
                                     for w in (w_raw, w_hi, w_lo))

        work = long_rows[:, :, :].rearrange("p a s -> p (a s)")
        proj = work[:, 0:3 * PAIR_COLS].rearrange("p (n c) -> p n c", n=3)
        at = 3 * PAIR_COLS
        by_cos = work[:, at:at + 2 * QK_COLS].rearrange("p (n c) -> p n c", n=2)
        at += 2 * QK_COLS
        by_sin = work[:, at:at + 2 * QK_COLS].rearrange("p (n c) -> p n c", n=2)
        at += 2 * QK_COLS
        roped = work[:, at:at + 4 * QK_COLS].rearrange("p (n h r d) -> p n h r d", n=2, h=4, r=2)

        def rows_of(j):
            t = TILE_OF[j]
            return (long_rows if t >= NT // 2 else short_rows)[:, t % 2, :]

        def pt_of(q):
            return (pt_short_hi, pt_short_lo) if q % 2 == 0 else (pt_long_hi, pt_long_lo)

        ps_s = ctx.enter_context(nc.psum_tensor("ps_s", [P, 3, BANK], F32))
        ps_t = ctx.enter_context(nc.psum_tensor("ps_t", [P, 3, BANK], F32))
        ps_o = ctx.enter_context(nc.psum_tensor("ps_o", [P, 2, BANK], F32))
        ps_v, ps_n = ps_o[:, :, 0:2 * P], ps_o[:, :, 2 * P:3 * P]

        consts_loaded = sem("consts_loaded")
        ones_ready = sem("ones_ready")
        x_loaded = [sem(f"x_loaded_{i}") for i in range(NX)]
        x_hi_ready = sem("x_hi_ready")
        x_lo_ready = sem("x_lo_ready")
        w_loaded = sem("w_loaded")
        w_hi_ready = sem("w_hi_ready")
        w_split = sem("w_split")
        piece_loaded = sem("piece_loaded")
        piece_split = sem("piece_split")
        piece_done = sem("piece_done")
        proj_done = sem("proj_done")
        proj_copied = sem("proj_copied")
        v_hi_ready = sem("v_hi_ready")
        v_lo_ready = sem("v_lo_ready")
        rope_mul = sem("rope_mul")
        rope_add = sem("rope_add")
        qk_turned = sem("qk_turned")
        qk_hi_ready = sem("qk_hi_ready")
        qk_lo_ready = sem("qk_lo_ready")
        bias_built = sem("bias_built")
        bias_masked = sem("bias_masked")
        scored = sem("scored")
        biased = sem("biased")
        exped = sem("exped")
        pt_turned = sem("pt_turned")
        pt_hi_ready = sem("pt_hi_ready")
        pt_lo_ready = sem("pt_lo_ready")
        pt_zeroed = sem("pt_zeroed")
        pv_done = sem("pv_done")
        o_copied = sem("o_copied")
        folded = sem("folded")
        inverted = sem("inverted")
        normed = sem("normed")
        stored = [sem("stored_even"), sem("stored_odd")]

        sp_passed, pool_passed, dve_passed, pe_passed = (sem(f"{e}_passed") for e in ("sp", "pool", "dve", "pe"))

        n_consts = 7
        S_ALL, T_ALL = S_SUM[TILES], T_SUM[TILES]
        BIAS_PER = 4
        LOW = 6 * P
        block = ctx.enter_context(nc.Block())

        @block.sync
        def _(sp):
            def load_piece(b, p, r):
                sp.dma_start(piece, ins["slabs"][3 * p + 2 + r, :, bass.ds(b * PIECE, PIECE)]) \
                    .then_inc(piece_loaded, 16)

            def load_w(pair):
                sp.dma_start(w_raw[:], ins["w_qkv"][pair]).then_inc(w_loaded, 16)
                sp.dma_start(b_raw[0:1, :], ins["b_qkv"][pair]).then_inc(w_loaded, 16)
                sp.dma_start(b_raw[32:33, :], ins["b_qkv"][pair]).then_inc(w_loaded, 16)

            sp.wait_ge(ones_ready, 1)
            load_w(0)
            with sp.Fori(0, B) as b:
                for i in range(NX):
                    cols = slice(i * XC, (i + 1) * XC)
                    sp.dma_start(long_rows[:, :, cols], ins["x_t"][b, :, :, cols]).then_inc(x_loaded[i], 16)
                with sp.Fori(0, PAIRS) as p:
                    it = b * PAIRS + p
                    sp.wait_ge(w_split, it + 1)
                    load_piece(b, p, 0)
                    for q in range(GROUPS):
                        if q in (1, 3):
                            sp.wait_ge(piece_split, (it * PIECES + q // 2 + 1) * 2)
                            load_piece(b, p, q // 2 + 1)
                        if q == 5:
                            sp.wait_ge(piece_split, (it + 1) * PIECES * 2)
                            load_w(p + 1)
                        sp.wait_ge(normed, it * GROUPS + q + 1)
                        hold(sp, sp_passed)
                        first = TILE_OF[2 * q]
                        dst = attn_dram[bass.ds(b * NT + first, 2), :, 2 * p + HEAD_OF[2 * q], :]
                        sp.dma_start(dst.rearrange("t p d -> p t d"), o_nat[:, q % 2, :, :]) \
                            .then_inc(stored[q % 2], 16)
                    sp.wait_ge(pt_turned, (it + 1) * T_ALL)
                    hold(sp, sp_passed)
            for par in range(2):
                sp.wait_ge(stored[par], 16 * (B * PAIRS * GROUPS // 2 + 1))
            sp.wait_ge(w_loaded, 48 * (B * PAIRS + 1))
            sp.wait_ge(piece_loaded, 16 * B * PAIRS * PIECES)

        @block.gpsimd
        def _(pool):
            pool.memset(b_raw[:], 0.0)
            pool.memset(b_st[:].bitcast(F32), 0.0)
            pool.memset(ones[:].bitcast(F32), 0.0)
            pool.drain()
            pool.memset(ones[0:1, :].bitcast(F32), 1.0)
            pool.drain()
            pool.memset(ones[32:33, :].bitcast(F32), 1.0).then_inc(ones_ready, 1)

            def split_w(lots):
                pool.wait_ge(w_loaded, lots * 48)
                hold(pool, pool_passed)
                pool.tensor_copy(w_hi[:], w_raw[:])
                pool.tensor_copy(b_hi[:], b_raw[:])
                pool.tensor_copy(b_st[0:1, :], b_raw[0:1, :]).then_inc(w_hi_ready, 1)
                pool.wait_ge(w_hi_ready, lots * 2 - 1)
                pool.tensor_tensor(w_lo[:], w_raw[:], w_hi[:].bitcast(F32), ALU.subtract).then_inc(w_hi_ready, 1)
                pool.wait_ge(w_hi_ready, lots * 2)
                pool.tensor_tensor(b_st[32:33, :], b_raw[32:33, :], b_hi[32:33, :].bitcast(F32),
                                   ALU.subtract).then_inc(w_split, 1)
                pool.wait_ge(w_split, lots)
                hold(pool, pool_passed)

            def split_piece(it, r):
                n = it * PIECES + r
                pool.wait_ge(piece_loaded, (n + 1) * 16)
                if r:
                    pool.wait_ge(piece_done, n)
                hold(pool, pool_passed)
                pool.tensor_copy(piece_hi, piece).then_inc(piece_split, 1)
                pool.wait_ge(piece_split, n * 2 + 1)
                pool.tensor_tensor(piece_lo, piece, piece_hi.bitcast(F32), ALU.subtract).then_inc(piece_split, 1)

            pool.wait_ge(ones_ready, 1)
            split_w(1)
            pool.wait_ge(consts_loaded, 16 * n_consts)
            with pool.Fori(0, B * PAIRS) as it:
                for t in range(NT):
                    pool.wait_ge(proj_copied, it * NT + t + 1)
                    if t >= 2:
                        pool.wait_ge(rope_add, it * NT + t - 1)
                    src = proj[:, t % 3, 0:QK_COLS].rearrange("p (h r d) -> p h r d", h=4, r=2)
                    cos_t = cos[:, t, :].rearrange("p (a b d) -> p a b d", a=1, b=1)
                    pool.tensor_tensor(by_cos[:, t % 2, :].rearrange("p (h r d) -> p h r d", h=4, r=2),
                                       src, cos_t.to_broadcast([P, 4, 2, HALF]), ALU.mult)
                    for r in range(2):
                        sin_t = sin[:, t, r * HALF:(r + 1) * HALF].rearrange("p (a d) -> p a d", a=1)
                        out = by_sin[:, t % 2, :].rearrange("p (h r d) -> p h r d", h=4, r=2)[:, :, r, :]
                        last = pool.tensor_tensor(out, src[:, :, 1 - r, :],
                                                  sin_t.to_broadcast([P, 4, HALF]), ALU.mult)
                    last.then_inc(rope_mul, 1)
                pool.wait_ge(proj_done, (it + 1) * NT)
                hold(pool, pool_passed)
                for q in range(GROUPS):
                    last_key = TILE_OF[2 * q] + 1
                    if q >= 2:
                        pool.wait_ge(pv_done, it * GROUPS + q - 1)
                        hold(pool, pool_passed)
                    hi, lo = pt_of(q)
                    pool.memset(hi[:, last_key, 0:P].bitcast(F32), 0.0)
                    pool.memset(lo[:, last_key, 0:P].bitcast(F32), 0.0).then_inc(pt_zeroed, 1)
                    if q in (1, 2, 4):
                        split_piece(it, q // 2)
                    if q == 7:
                        pool.wait_ge(piece_done, (it + 1) * PIECES)
                        split_w(it + 2)

        @block.scalar
        def _(act):
            for dst, src in ((ident, "ident"), (cos, "cos"), (sin, "sin"), (rel, "rel"), (slopes, "slopes"),
                             (mask, "mask"), (fold, "fold")):
                act.dma_start(dst[:], ins[src]).then_inc(consts_loaded, 16)

            def build_bias(it, head, lo, hi):
                act.activation(bias_t[:, lo:hi], rel[:, lo:hi], ACT.Copy,
                               scale=slopes[:, bass.ds(it * 2 + head, 1)]).then_inc(bias_built, 1)

            act.preload_act_table(ACT.Exp)
            with act.Fori(0, B * PAIRS, PAIRS) as b0:
                for i in range(NX):
                    cols = slice(i * XC, (i + 1) * XC)
                    act.wait_ge(x_loaded[i], b0 * (16 // PAIRS) + 16)
                    act.activation(x_hi[:, :, cols], long_rows[:, :, cols], ACT.Copy).then_inc(x_hi_ready, PAIRS)
                act.wait_ge(consts_loaded, 16 * n_consts)
                with act.Fori(b0, b0 + PAIRS) as it:
                    for step in range(NT + 2):
                        t = step
                        if t < NT:
                            act.wait_ge(proj_done, it * NT + t + 1)
                            if t == 0:
                                act.wait_ge(x_lo_ready, b0 * NX + NX * PAIRS)
                            if t >= 3:
                                act.wait_ge(rope_mul, it * NT + t - 2)
                                act.wait_ge(v_lo_ready, it * NT + t - 2)
                            act.activation(proj[:, t % 3, :], ps_s[:, t % 3, 0:PAIR_COLS], ACT.Copy) \
                                .then_inc(proj_copied, 1)
                            act.wait_ge(proj_copied, it * NT + t + 1)
                            act.activation(v_st[:, :, t, 0:DH],
                                           proj[:, t % 3, QK_COLS:PAIR_COLS].rearrange("p (h d) -> p h d", h=2),
                                           ACT.Copy).then_inc(v_hi_ready, 1)
                            if t in (6, 10):
                                build_bias(it, 0, 0 if t == 6 else S // 2, S // 2 if t == 6 else S)
                        t = step - 2
                        if t >= 0:
                            act.wait_ge(qk_turned, it * NT + t + 1)
                            turned = ps_t[:, t % 3, :].rearrange("p (h c) -> p h c", h=4)
                            act.activation(q_st[:, :, t * P:(t + 1) * P], turned[:, 0:2, :], ACT.Copy,
                                           scale=Q_SCALE)
                            act.activation(k_hi[:, :, t * P:(t + 1) * P], turned[:, 2:4, :], ACT.Copy) \
                                .then_inc(qk_hi_ready, 1)

                    def exp(j):
                        width = P * (TILE_OF[j] + 1)
                        act.wait_ge(biased, it * S_ALL + S_SUM[j + 1])
                        rows = rows_of(j)[:, 0:width]
                        n = len(s_chunks(j)) - 1
                        act.activation(rows, rows, ACT.Exp, bias=row_min[:, j, n:n + 1], scale=-1.0,
                                       accum_out=row_sum[:, j:j + 1]).then_inc(exped, 1)

                    def pt_high(j, c):
                        k0, n = t_chunks(j)[c]
                        i = T_SUM[j] + c
                        q = j // 2
                        if c == 0 and q >= 2:
                            act.wait_ge(pv_done, it * GROUPS + q - 1)
                        act.wait_ge(pt_turned, it * T_ALL + i + 1)
                        act.activation(pt_of(q)[0][:, k0:k0 + n, (j % 2) * P:(j % 2 + 1) * P],
                                       ps_t[:, bank(i), 0:n * P].rearrange("p (k c) -> p k c", k=n),
                                       ACT.Copy).then_inc(pt_hi_ready, 1)

                    for j in range(AHEAD - 1):
                        exp(j)
                    for j in range(TILES + 3):
                        if j >= 4 and j % 2 == 0:
                            q = (j - 4) // 2
                            act.wait_ge(pv_done, it * GROUPS + q + 1)
                            if q >= 2:
                                act.wait_ge(folded, it * GROUPS + q - 1)
                            act.activation(o_sb[:, q % 2, :], ps_v[:, q % 2, :], ACT.Copy).then_inc(o_copied, 1)
                        if j < TILES:
                            n = len(t_chunks(j))
                            for c in range(n):
                                pt_high(j, c)
                            if j + AHEAD - 1 < TILES:
                                exp(j + AHEAD - 1)
                            if j + AHEAD - 1 == NT - 4:
                                act.wait_ge(biased, it * S_ALL + S_SUM[NT - 4])
                                build_bias(it, 1, 0, LOW)
                            if j + AHEAD - 1 == NT - 1:
                                build_bias(it, 1, LOW, S)

        @block.vector
        def _(dve):
            for par in range(2):
                dve.memset(o_nat[:, par, :, :], 0.0).then_inc(stored[par], 16)
            with dve.Fori(0, B * PAIRS, PAIRS) as b0:
                for i in range(NX):
                    cols = slice(i * XC, (i + 1) * XC)
                    dve.wait_ge(x_hi_ready, b0 * NX + (i + 1) * PAIRS)
                    dve.tensor_tensor(x_lo[:, :, cols], long_rows[:, :, cols], x_hi[:, :, cols].bitcast(F32),
                                      ALU.subtract).then_inc(x_lo_ready, PAIRS)
                dve.wait_ge(consts_loaded, 16 * n_consts)
                with dve.Fori(b0, b0 + PAIRS) as it:
                    def mask_bias(n):
                        dve.wait_ge(bias_built, it * BIAS_PER + n)
                        dve.tensor_tensor(bias_t[:, S - P:S], bias_t[:, S - P:S], mask[:], ALU.add) \
                            .then_inc(bias_masked, 1)

                    def add_bias(j, chunks):
                        if j == NT and 0 in chunks:
                            mask_bias(4)
                        for c, (k0, width) in enumerate(s_chunks(j)):
                            if c not in chunks:
                                continue
                            i = S_SUM[j] + c
                            if c == 0:
                                if j >= 4:
                                    dve.wait_ge(pt_turned, it * T_ALL + T_SUM[j - 3])
                                dve.wait_ge(bias_masked, it * 2 + HEAD_OF[j] + 1)
                            else:
                                dve.wait_ge(biased, it * S_ALL + i)
                            dve.wait_ge(scored, it * S_ALL + i + 1)
                            hold(dve, dve_passed)
                            off = S - P - P * TILE_OF[j] + k0
                            dve.tensor_tensor_reduce(
                                rows_of(j)[:, k0:k0 + width], ps_s[:, bank(i), 0:width], bias_t[:, off:off + width],
                                1.0, 3.0e38 if c == 0 else row_min[:, j, c - 1:c], ALU.add, ALU.min,
                                row_min[:, j, c:c + 1]).then_inc(biased, 1)

                    for step in range(NT + 2):
                        t = step - 1
                        if 0 <= t < NT:
                            dve.wait_ge(rope_mul, it * NT + t + 1)
                            if t >= 2:
                                dve.wait_ge(qk_turned, it * NT + t - 1)
                            shape = [P, 4, 2, DH]
                            dve.tensor_tensor(
                                roped[:, t % 2],
                                by_cos[:, t % 2, :].rearrange("p (h r d) -> p h r d", h=4, r=1).to_broadcast(shape),
                                by_sin[:, t % 2, :].rearrange("p (h r d) -> p h r d", h=4, r=1).to_broadcast(shape),
                                ALU.add).then_inc(rope_add, 1)
                            dve.wait_ge(v_hi_ready, it * NT + t + 1)
                            dve.tensor_tensor(v_st[:, :, t, DH:2 * DH],
                                              proj[:, t % 3, QK_COLS:PAIR_COLS].rearrange("p (h d) -> p h d", h=2),
                                              v_st[:, :, t, 0:DH].bitcast(F32), ALU.subtract).then_inc(v_lo_ready, 1)
                        t = step - 2
                        if t == 11:
                            mask_bias(2)
                        if t >= 0:
                            dve.wait_ge(qk_hi_ready, it * NT + t + 1)
                            turned = ps_t[:, t % 3, :].rearrange("p (h c) -> p h c", h=4)
                            cols = slice(t * P, (t + 1) * P)
                            dve.scalar_tensor_tensor(q_st[DH:P, :, cols], turned[DH:P, 0:2, :], Q_SCALE,
                                                     q_st[DH:P, :, cols].bitcast(F32), ALU.mult, ALU.subtract)
                            dve.tensor_tensor(k_lo[:, :, cols], turned[:, 2:4, :],
                                              k_hi[:, :, cols].bitcast(F32), ALU.subtract) \
                                .then_inc(qk_lo_ready, 1)
                        if step == NT:
                            add_bias(0, range(4))
                            add_bias(1, range(4))

                    def pt_low(j, c):
                        k0, n = t_chunks(j)[c]
                        i = T_SUM[j] + c
                        hi, lo = pt_of(j // 2)
                        cols = slice((j % 2) * P, (j % 2 + 1) * P)
                        dve.wait_ge(pt_hi_ready, it * T_ALL + i + 1)
                        dve.tensor_tensor(lo[:, k0:k0 + n, cols],
                                          ps_t[:, bank(i), 0:n * P].rearrange("p (k c) -> p k c", k=n),
                                          hi[:, k0:k0 + n, cols].bitcast(F32), ALU.subtract) \
                            .then_inc(pt_lo_ready, 1)

                    dve.wait_ge(v_lo_ready, (it + 1) * NT)
                    add_bias(2, range(4))
                    def norm(q):
                        dve.wait_ge(exped, it * TILES + 2 * q + 2)
                        dve.reciprocal(row_inv[:, 2 * q:2 * q + 2], row_sum[:, 2 * q:2 * q + 2]) \
                            .then_inc(inverted, 1)
                        dve.wait_ge(folded, it * GROUPS + q + 1)
                        dve.wait_ge(stored[q % 2], (it * (GROUPS // 2) + q // 2 + 1) * 16)
                        dve.wait_ge(inverted, it * GROUPS + q + 1)
                        inv = row_inv[:, 2 * q:2 * q + 2].rearrange("p (t a) -> p t a", a=1)
                        dve.tensor_tensor(o_nat[:, q % 2, :, :],
                                          ps_n[:, q % 2, :].rearrange("p (t d) -> p t d", t=2),
                                          inv.to_broadcast([P, 2, DH]), ALU.mult).then_inc(normed, 1)

                    for j in range(TILES + 3):
                        n = len(t_chunks(j)) if j < TILES else 0
                        for r in range(4):
                            if j + AHEAD < TILES:
                                add_bias(j + AHEAD, range(r, r + 1))
                            if r < n:
                                pt_low(j, r)
                        if j >= 4 and j % 2 == 0:
                            norm((j - 4) // 2)
                        if j in (4, 8, 12):
                            n = it * PIECES + j // 4 - 1
                            dve.wait_ge(piece_split, n * 2 + 2)
                            hold(dve, dve_passed)
                            dve.tensor_reduce(lo_max[:, bass.ds(n, 1)], piece_lo.bitcast(F32),
                                              mybir.AxisListType.X, ALU.max,
                                              apply_absolute_value=True).then_inc(piece_done, 1)

        @block.tensor
        def _(pe):
            pe.wait_ge(consts_loaded, 16 * n_consts)
            pe.wait_ge(ones_ready, 1)
            with pe.Fori(0, B * PAIRS, PAIRS) as b0:
                def project(it, t):
                    if t % (NT // NX) == 0:
                        pe.wait_ge(x_lo_ready, b0 * NX + (t * NX // NT + 1) * PAIRS)
                    if t >= 3:
                        pe.wait_ge(proj_copied, it * NT + t - 2)
                    out = ps_s[:, t % 3, 0:PAIR_COLS]
                    rows = slice(t * P, (t + 1) * P)
                    pe.matmul(out, ones[:], b_st[:], start=True, stop=False)
                    for k in range(KD):
                        pe.matmul(out, x_hi[:, k, rows], w_hi[:, k, :], start=False, stop=False)
                        pe.matmul(out, x_hi[:, k, rows], w_lo[:, k, :], start=False, stop=False)
                        last = pe.matmul(out, x_lo[:, k, rows], w_hi[:, k, :], start=False, stop=k == KD - 1)
                    last.then_inc(proj_done, 1)

                pe.wait_ge(w_split, b0 + 1)
                for t in range(3):
                    project(b0, t)
                with pe.Fori(b0, b0 + PAIRS) as it:
                    def score(j, chunks):
                        head, rows = HEAD_OF[j], slice(TILE_OF[j] * P, (TILE_OF[j] + 1) * P)
                        for c, (k0, width) in enumerate(s_chunks(j)):
                            if c not in chunks:
                                continue
                            i = S_SUM[j] + c
                            if i >= 3:
                                pe.wait_ge(biased, it * S_ALL + i - 2)
                            else:
                                pe.wait_ge(proj_copied, it * NT + NT - 2 + i)
                            n = max(2 * P, width)
                            out = ps_s[:, bank(i), 0:n]
                            pe.matmul(out, q_st[:, head, rows], k_hi[:, head, k0:k0 + n], start=True, stop=False)
                            pe.matmul(out, q_st[:, head, rows], k_lo[:, head, k0:k0 + n],
                                      start=False, stop=True).then_inc(scored, 1)

                    for step in range(3, NT + 2):
                        if step < NT:
                            project(it, step)
                        if step == NT:
                            pe.wait_ge(qk_lo_ready, it * NT + 2)
                            score(0, range(4))
                            score(1, range(4))
                        for t in ((0, 1) if step == 3 else (step - 2,)):
                            pe.wait_ge(rope_add, it * NT + t + 1)
                            if t >= 3:
                                pe.wait_ge(qk_lo_ready, it * NT + t - 2)
                            for h in range(4):
                                src = roped[:, t % 2, h].rearrange("p r d -> p (r d)")
                                last = pe.transpose(ps_t[:, t % 3, h * P:(h + 1) * P], src, ident[:])
                            last.then_inc(qk_turned, 1)

                    def turn(j, c):
                        k0, n = t_chunks(j)[c]
                        i = T_SUM[j] + c
                        if i >= 3:
                            pe.wait_ge(pt_lo_ready, it * T_ALL + i - 2)
                        if c == 0:
                            pe.wait_ge(exped, it * TILES + j + 1)
                        for k in range(n):
                            last = pe.transpose(ps_t[:, bank(i), k * P:(k + 1) * P],
                                                rows_of(j)[:, (k0 + k) * P:(k0 + k + 1) * P], ident[:])
                        last.then_inc(pt_turned, 1)

                    def weigh(q, half, quarter):
                        keys = TILE_OF[2 * q] + 2
                        head = HEAD_OF[2 * q]
                        hi, lo = pt_of(q)
                        if half == 0 and quarter == 0:
                            pe.wait_ge(pt_lo_ready, it * T_ALL + T_SUM[2 * q + 2])
                            pe.wait_ge(pt_zeroed, it * GROUPS + q + 1)
                            if q >= 2:
                                pe.wait_ge(normed, it * GROUPS + q - 1)
                        first = half * keys // 2
                        for k in range(first + quarter * keys // 8, first + (quarter + 1) * keys // 8):
                            for part in (hi, lo):
                                last = pe.matmul(ps_v[:, q % 2, :], v_st[:, head, k, :], part[:, k, :],
                                                 start=k == 0 and part is hi, stop=k == keys - 1 and part is lo)
                                if k == keys - 1 and part is lo:
                                    last.then_inc(pv_done, 1)

                    def add_parts(q):
                        pe.wait_ge(o_copied, it * GROUPS + q + 1)
                        for r in range(2):
                            last = pe.matmul(ps_n[:, q % 2, r * DH:(r + 1) * DH], o_sb[:, q % 2, r * P:(r + 1) * P],
                                             fold[:], start=True, stop=True)
                        last.then_inc(folded, 1)

                    pe.wait_ge(qk_lo_ready, it * NT + NT - 1)
                    score(2, range(3))
                    pe.wait_ge(v_lo_ready, (it + 1) * NT)
                    pe.wait_ge(qk_lo_ready, (it + 1) * NT)
                    score(2, range(3, 4))
                    for j in range(TILES + 3):
                        n = len(t_chunks(j)) if j < TILES else 0
                        for r in range(4):
                            if j + AHEAD < TILES:
                                score(j + AHEAD, range(r, r + 1))
                            if r < n:
                                turn(j, r)
                            if r == 1 and 4 <= j < TILES + 2 and j % 2 == 0:
                                add_parts((j - 4) // 2)
                        if j >= TILES:
                            with pe.If(it < b0 + PAIRS - 1):
                                if j == TILES:
                                    pe.wait_ge(biased, (it + 1) * S_ALL)
                                    pe.wait_ge(w_split, it + 2)
                                    hold(pe, pe_passed)
                                project(it + 1, j - TILES)
                        if j == TILES + 2:
                            add_parts(GROUPS - 1)
                        if 2 <= j < TILES + 2:
                            for r in range(4):
                                weigh((j - 2) // 2, j % 2, r)


SLABS = 2 + MT // 2 + 2 * MT + 2
SLAB = 1024
RING = 3
SLAB_UP, SLAB_HID, SLAB_DOWN = 2, 2 + MT // 2, 2 + MT // 2 + 2 * MT
HALVES = TOK // BANK


def feed_forward(nc, ins, attn_dram, lo_max, out):
    ctx = ExitStack()
    with ctx:
        def sb(name, shape, dt=F32):
            return ctx.enter_context(nc.sbuf_tensor(name, shape, dt))

        def sem(name):
            return ctx.enter_context(nc.semaphore(name))

        slab_raw = sb("slab_raw", [P, RING, SLAB])
        slab_hi = sb("slab_hi", [P, RING, SLAB], F32R)
        slab_lo = sb("slab_lo", [P, RING, SLAB], F32R)
        y_nat = sb("y_nat", [P, TT, DM])
        y_hi = sb("y_hi", [P, KD, TOK], F32R)
        y_lo = sb("y_lo", [P, KD, TOK], F32R)
        ha_hi = sb("ha_hi", [P, MT, TOK], F32R)
        ha_lo = sb("ha_lo", [P, MT, TOK], F32R)
        hb_hi = sb("hb_hi", [P, MT, TOK], F32R)
        hb_lo = sb("hb_lo", [P, MT, TOK], F32R)
        silu = sb("silu", [P, 2, BANK])
        hid = sb("hid", [P, 2, BANK])
        ident = sb("ident_f", [P, P])
        s_hid = sb("s_hid", [P, 4, MT])
        b_out = sb("b_out", [P, DM])
        s_down = sb("s_down", [P, DM])
        eps = sb("eps", [P, 1])
        stats = sb("stats", [P, TT, 6])
        moments = sb("moments", [P, TT, 2])
        std = sb("std", [P, TT])
        rstd = sb("rstd", [P, TT])
        largest_lo = sb("largest_lo", [P, 1])
        has_lo = sb("has_lo", [P, 1])
        ones = sb("ones_f", [P, 1])
        rows_with_lo = sb("rows_with_lo", [1, 1], I32)

        attn = hb_lo[:].bitcast(F32)
        at_hi, at_lo = hb_hi, ha_lo

        ps_m = ctx.enter_context(nc.psum_tensor("ps_m", [P, 4, BANK], F32))
        ps_acc = ctx.enter_context(nc.psum_tensor("ps_acc", [P, TT, DM], F32))

        consts_loaded = sem("f_consts_loaded")
        eps_ready = sem("eps_ready")
        flag_step = sem("flag_step")
        raw_loaded = [sem(f"raw_loaded_{i}") for i in range(RING)]
        slab_hi_ready = sem("slab_hi_ready")
        slab_ready = sem("slab_ready")
        slab_used = sem("slab_used")
        x_loaded = [sem("f_x_loaded_a"), sem("f_x_loaded_b")]
        x_biased = sem("x_biased")
        attn_loaded = [sem(f"attn_loaded_{i}") for i in range(TT // 2)]
        attn_turned = sem("attn_turned")
        attn_hi_ready = sem("attn_hi_ready")
        attn_lo_ready = sem("attn_lo_ready")
        acc_done = sem("acc_done")
        step_done = sem("step_done")
        var_ready = sem("var_ready")
        std_ready = sem("std_ready")
        y_ready = sem("y_ready")
        y_turned = sem("y_turned")
        y_hi_ready = sem("y_hi_ready")
        y_lo_ready = sem("y_lo_ready")
        up_done = sem("up_done")
        silu_ready = sem("silu_ready")
        gated = sem("gated")
        up_hi_ready = sem("up_hi_ready")
        up_lo_ready = sem("up_lo_ready")
        hid_done = sem("hid_done")
        gelu_ready = sem("gelu_ready")
        hid_hi_ready = sem("hid_hi_ready")
        hid_lo_ready = sem("hid_lo_ready")
        out_ready = sem("out_ready")
        out_stored = [sem("out_stored_a"), sem("out_stored_b")]

        sp_passed, pool_passed, dve_passed = (sem(f"f_{e}_passed") for e in ("sp", "pool", "dve"))

        HT = TT // 2
        tokens = "(c g t p) d -> c g p t d"
        x_rows = ins["x"].rearrange("b s d -> (b s) d").rearrange(tokens, g=2, t=HT, p=P)
        out_rows = out.rearrange("b s d -> (b s) d").rearrange(tokens, g=2, t=HT, p=P)
        attn_rows = attn_dram.rearrange("(c i t) p h d -> c i p t (h d)", i=TT // 2, t=2)
        UP_UNITS = MT * HALVES
        HID_UNITS = 2 * MT * HALVES
        CHAIN = (4 + 6) * (TT // 2) + 4
        n_consts = 4

        def up_place(n):
            return n // 4 * 2 + n % 2, n % 4 // 2

        def up_units(m, half):
            return m // 2 * 4 + half * 2 + m % 2 + 1

        def hid_place(n):
            return n // UP_UNITS, n % UP_UNITS // HALVES, n % HALVES

        def load_attn(queue, c):
            for i in range(TT // 2):
                queue.dma_start(attn[:, 2 * i:2 * i + 2, :], attn_rows[c, i]).then_inc(attn_loaded[i], 16)

        def half_cols(half):
            return slice(half * BANK, (half + 1) * BANK)

        def tile_cols(t):
            return slice(t * P, (t + 1) * P)

        block = ctx.enter_context(nc.Block())

        @block.sync
        def _(sp):
            sp.dma_start(ident[:], ins["ident"]).then_inc(consts_loaded, 16)
            sp.dma_start(s_hid[:], ins["s_hid"]).then_inc(consts_loaded, 16)
            sp.dma_start(b_out[:], ins["b_out"].to_broadcast([P, DM])).then_inc(consts_loaded, 16)
            sp.dma_start(s_down[:], ins["s_down"].to_broadcast([P, DM])).then_inc(consts_loaded, 16)
            for s in range(RING):
                sp.dma_start(slab_raw[:, s, :], ins["slabs"][s]).then_inc(raw_loaded[s], 16)
                if s == 1:
                    load_attn(sp, 0)
            with sp.Fori(0, CHUNKS) as c:
                for g in range(2):
                    sp.dma_start(y_nat[:, g * HT:(g + 1) * HT, :], x_rows[c, g]).then_inc(x_loaded[g], 16)
                for s in range(SLABS):
                    sp.wait_ge(slab_ready, c * SLABS + s + 1)
                    sp.dma_start(slab_raw[:, s % RING, :], ins["slabs"][(s + RING) % SLABS]) \
                        .then_inc(raw_loaded[s % RING], 16)
                for g in range(2):
                    sp.wait_ge(out_ready, c * TT + (g + 1) * HT)
                    sp.dma_start(out_rows[c, g], y_nat[:, g * HT:(g + 1) * HT, :]).then_inc(out_stored[g], 16)
                for g in range(2):
                    sp.wait_ge(out_stored[g], c * 16 + 16)
                hold(sp, sp_passed)
            for g in range(2):
                sp.wait_ge(out_stored[g], CHUNKS * 16)
            for i in range(RING):
                sp.wait_ge(raw_loaded[i], 16 * (CHUNKS * SLABS // RING + 1))

        @block.gpsimd
        def _(pool):
            pool.memset(eps[:], EPS).then_inc(eps_ready, 1)

            def split(s, loads, lots):
                i = s % RING
                pool.wait_ge(raw_loaded[i], loads * 16)
                hold(pool, pool_passed)
                pool.tensor_copy(slab_hi[:, i, :], slab_raw[:, i, :]).then_inc(slab_hi_ready, 1)
                pool.wait_ge(slab_hi_ready, lots)
                pool.tensor_tensor(slab_lo[:, i, :], slab_raw[:, i, :],
                                   slab_hi[:, i, :].bitcast(F32), ALU.subtract).then_inc(slab_ready, 1)

            for s in range(RING):
                split(s, 1, s + 1)
            pool.wait_ge(consts_loaded, 16 * n_consts)
            with pool.Fori(0, CHUNKS) as c:
                for t in range(TT):
                    if t % HT == 0:
                        pool.wait_ge(x_loaded[t // HT], c * 16 + 16)
                    pool.tensor_tensor(y_nat[:, t, :], y_nat[:, t, :], b_out[:], ALU.add).then_inc(x_biased, 1)
                for s in range(SLABS):
                    pool.wait_ge(slab_used, c * SLABS + s + 1)
                    split(s, c * (SLABS // RING) + s // RING + 2, c * SLABS + s + RING + 1)

        @block.scalar
        def _(act):
            act.preload_act_table(ACT.Sqrt)
            act.wait_ge(eps_ready, 1)
            act.wait_ge(consts_loaded, 16 * n_consts)
            with act.Fori(0, CHUNKS) as c:
                def sqrt(n, g):
                    act.wait_ge(var_ready, (c * 2 + n) * TT + (g + 1) * HT)
                    act.activation(std[:, g * HT:(g + 1) * HT], moments[:, g * HT:(g + 1) * HT, 1], ACT.Sqrt,
                                   bias=eps[:]).then_inc(std_ready, 1)

                def y_high(u):
                    act.wait_ge(y_turned, c * (TT // 2) + u + 1)
                    act.activation(y_hi[:, :, u * 2 * P:(u + 1) * 2 * P].rearrange("p k (t c) -> p t k c", t=2),
                                   ps_acc[:, 2 * u:2 * u + 2, :].rearrange("p t (k c) -> p t k c", k=KD),
                                   ACT.Copy).then_inc(y_hi_ready, 1)

                for u in range(2 * TT):
                    t, k0 = u // 2, u % 2 * 4
                    act.wait_ge(attn_turned, c * 2 * TT + u + 1)
                    act.activation(at_hi[:, k0:k0 + 4, tile_cols(t)],
                                   ps_m[:, u % 4, :].rearrange("p (k c) -> p k c", k=4), ACT.Copy) \
                        .then_inc(attn_hi_ready, 1)
                sqrt(0, 0)
                y_high(0)
                y_high(1)
                sqrt(0, 1)
                act.preload_act_table(ACT.Silu)

                for n in range(UP_UNITS + 1):
                    if n == 2:
                        y_high(2)
                        y_high(3)
                    if n < UP_UNITS:
                        m, half = up_place(n)
                        act.wait_ge(up_done, c * UP_UNITS + n + 1)
                        if n >= 2:
                            act.wait_ge(gated, c * UP_UNITS + n - 1)
                        act.activation(silu[:, n % 2, :], ps_m[:, n % 2 * 2, :], ACT.Silu,
                                       scale=s_hid[:, 0, m:m + 1]).then_inc(silu_ready, 1)
                    else:
                        act.preload_act_table(ACT.Gelu)
                    if n >= 1:
                        m, half = up_place(n - 1)
                        act.wait_ge(gated, c * UP_UNITS + n)
                        act.activation(ha_hi[:, m, half_cols(half)], hid[:, (n - 1) % 2, :], ACT.Copy) \
                            .then_inc(up_hi_ready, 1)
                for n in range(HID_UNITS):
                    layer, m, half = hid_place(n)
                    act.wait_ge(hid_done, c * HID_UNITS + n + 1)
                    if n >= 2:
                        act.wait_ge(hid_lo_ready, c * HID_UNITS + n - 1)
                    else:
                        act.wait_ge(up_lo_ready, c * UP_UNITS + UP_UNITS - 1 + n)
                    act.activation(hid[:, n % 2, :], ps_m[:, n % 4, :], ACT.Gelu,
                                   scale=s_hid[:, 2 + layer, m:m + 1]).then_inc(gelu_ready, 1)
                    act.wait_ge(gelu_ready, c * HID_UNITS + n + 1)
                    act.activation((ha_hi if layer else hb_hi)[:, m, half_cols(half)], hid[:, n % 2, :], ACT.Copy) \
                        .then_inc(hid_hi_ready, 1)
                with act.If(c < CHUNKS - 1):
                    load_attn(act, c + 1)
                act.preload_act_table(ACT.Sqrt)
                sqrt(1, 0)
                sqrt(1, 1)

        @block.vector
        def _(dve):
            dve.memset(ones[:], 1.0)
            dve.tensor_reduce(largest_lo[:], lo_max[:, 0:B * PAIRS * PIECES], mybir.AxisListType.X, ALU.max,
                              apply_absolute_value=True).then_inc(flag_step, 1)
            dve.wait_ge(flag_step, 1)
            dve.tensor_scalar(has_lo[:], largest_lo[:], 0.0, None, ALU.is_gt).then_inc(flag_step, 1)
            dve.wait_ge(flag_step, 3)
            dve.tensor_copy(rows_with_lo[:], ps_m[0:1, 0, 0:1]).then_inc(flag_step, 1)
            dve.wait_ge(consts_loaded, 16 * n_consts)
            with dve.Fori(0, CHUNKS) as c:
                steps = [0]
                stats_step = {}

                def chained(op):
                    steps[0] += 1
                    op.then_inc(step_done, 1)
                    return steps[0]

                def wait_step(n):
                    dve.wait_ge(step_done, c * CHAIN + n)

                def attn_low(t):
                    for u in (2 * t, 2 * t + 1):
                        k0 = u % 2 * 4
                        dve.wait_ge(attn_hi_ready, c * 2 * TT + u + 1)
                        dve.tensor_tensor(at_lo[:, k0:k0 + 4, tile_cols(t)],
                                          ps_m[:, u % 4, :].rearrange("p (k c) -> p k c", k=4),
                                          at_hi[:, k0:k0 + 4, tile_cols(t)].bitcast(F32), ALU.subtract) \
                            .then_inc(attn_lo_ready, 1)

                def pair_stats(added, tiles):
                    for t in tiles:
                        wait_step(added[t])
                        stats_step[t] = chained(dve.bn_stats(stats[:, t, :], y_nat[:, t, :]))

                def add_x(pair):
                    tiles = (2 * pair, 2 * pair + 1)
                    dve.wait_ge(acc_done, c * 2 * TT + tiles[1] + 1)
                    added = {}
                    for t in tiles:
                        dve.wait_ge(x_biased, c * TT + t + 1)
                        added[t] = chained(dve.tensor_tensor(y_nat[:, t, :], ps_acc[:, t, :], y_nat[:, t, :], ALU.add))
                    pair_stats(added, tiles)

                def add_y(pair):
                    tiles = (2 * pair, 2 * pair + 1)
                    dve.wait_ge(acc_done, c * 2 * TT + TT + tiles[1] + 1)
                    scaled, added = {}, {}
                    for t in tiles:
                        scaled[t] = chained(dve.tensor_tensor(silu[:, t % 2, 0:DM], ps_acc[:, t, :], s_down[:],
                                                              ALU.mult))
                    for t in tiles:
                        wait_step(scaled[t])
                        added[t] = chained(dve.tensor_tensor(y_nat[:, t, :], silu[:, t % 2, 0:DM], y_nat[:, t, :],
                                                             ALU.add))
                    pair_stats(added, tiles)

                def moments_of(g):
                    for t in range(g * HT, (g + 1) * HT):
                        wait_step(stats_step[t])
                        hold(dve, dve_passed)
                        dve.bn_aggr(moments[:, t, :], stats[:, t, :]).then_inc(var_ready, 1)

                def normalize(n, g, ready):
                    half = slice(g * HT, (g + 1) * HT)
                    dve.wait_ge(std_ready, c * 4 + n * 2 + g + 1)
                    wait_step(chained(dve.reciprocal(rstd[:, half], std[:, half])))
                    for t in range(g * HT, (g + 1) * HT):
                        dve.tensor_scalar(y_nat[:, t, :], y_nat[:, t, :], moments[:, t, 0:1], rstd[:, t:t + 1],
                                          ALU.subtract, ALU.mult).then_inc(ready, 1)

                def y_low(u):
                    dve.wait_ge(y_hi_ready, c * (TT // 2) + u + 1)
                    view = lambda a: a[:, :, u * 2 * P:(u + 1) * 2 * P].rearrange("p k (t c) -> p t k c", t=2)
                    dve.tensor_tensor(view(y_lo), ps_acc[:, 2 * u:2 * u + 2, :].rearrange("p t (k c) -> p t k c", k=KD),
                                      view(y_hi).bitcast(F32), ALU.subtract).then_inc(y_lo_ready, 1)

                attn_low(0)
                attn_low(1)
                for t in range(2, TT):
                    attn_low(t)
                    if t == 4:
                        add_x(0)
                    if t == 6:
                        add_x(1)
                        moments_of(0)
                normalize(0, 0, y_ready)
                add_x(2)
                y_low(0)
                y_low(1)
                add_x(3)
                moments_of(1)
                normalize(0, 1, y_ready)
                for n in range(UP_UNITS + 1):
                    if n == 2:
                        y_low(2)
                        y_low(3)
                    if n < UP_UNITS:
                        m, half = up_place(n)
                        if n >= 2:
                            dve.wait_ge(up_lo_ready, c * UP_UNITS + n - 1)
                        dve.wait_ge(silu_ready, c * UP_UNITS + n + 1)
                        dve.scalar_tensor_tensor(hid[:, n % 2, :], ps_m[:, n % 2 * 2 + 1, :], s_hid[:, 1, m:m + 1],
                                                 silu[:, n % 2, :], ALU.mult, ALU.mult).then_inc(gated, 1)
                    if n >= 1:
                        m, half = up_place(n - 1)
                        dve.wait_ge(up_hi_ready, c * UP_UNITS + n)
                        dve.tensor_tensor(ha_lo[:, m, half_cols(half)], hid[:, (n - 1) % 2, :],
                                          ha_hi[:, m, half_cols(half)].bitcast(F32), ALU.subtract) \
                            .then_inc(up_lo_ready, 1)
                for n in range(HID_UNITS):
                    layer, m, half = hid_place(n)
                    dve.wait_ge(hid_hi_ready, c * HID_UNITS + n + 1)
                    dve.tensor_tensor((ha_lo if layer else hb_lo)[:, m, half_cols(half)], hid[:, n % 2, :],
                                      (ha_hi if layer else hb_hi)[:, m, half_cols(half)].bitcast(F32),
                                      ALU.subtract).then_inc(hid_lo_ready, 1)
                for g in range(2):
                    add_y(2 * g)
                    add_y(2 * g + 1)
                    moments_of(g)
                    normalize(1, g, out_ready)
                assert steps[0] == CHAIN, steps[0]

        @block.tensor
        def _(pe):
            def chunk(c, lo_weights):
                def turn_attn(t):
                    if t % 2 == 0:
                        pe.wait_ge(attn_loaded[t // 2], c * 16 + 16)
                    for u in (2 * t, 2 * t + 1):
                        if u >= 4:
                            pe.wait_ge(attn_lo_ready, c * 2 * TT + u - 3)
                        for k in range(4):
                            last = pe.transpose(ps_m[:, u % 4, k * P:(k + 1) * P],
                                                attn[:, t, (u % 2 * 4 + k) * P:(u % 2 * 4 + k + 1) * P], ident[:])
                        last.then_inc(attn_turned, 1)

                def rows_out(t, s, half, hi, lo, with_lo):
                    for kk in range(4):
                        k = half * 4 + kk
                        wh = slab_hi[:, s % RING, kk * DM:(kk + 1) * DM]
                        wl = slab_lo[:, s % RING, kk * DM:(kk + 1) * DM]
                        pe.matmul(ps_acc[:, t, :], hi[:, k, tile_cols(t)], wh, start=k == 0 and t % 2 == 0,
                                  stop=False, skip_group_check=True)
                        if with_lo:
                            pe.matmul(ps_acc[:, t, :], hi[:, k, tile_cols(t)], wl, start=False, stop=False,
                                      skip_group_check=True)
                        last = pe.matmul(ps_acc[:, t, :], lo[:, k, tile_cols(t)], wh, start=False,
                                         stop=k == MT - 1, skip_group_check=True)
                    if half:
                        last.then_inc(acc_done, 1)

                def turn_y(u):
                    pe.wait_ge(y_ready, c * TT + 2 * u + 2)
                    for t in (2 * u, 2 * u + 1):
                        for k in range(KD):
                            last = pe.transpose(ps_acc[:, t, k * P:(k + 1) * P], y_nat[:, t, k * P:(k + 1) * P],
                                                ident[:])
                    last.then_inc(y_turned, 1)

                def product(out, s, at, hi, lo, half, tiles, inputs_ready=None):
                    for k in range(tiles):
                        if inputs_ready:
                            inputs_ready(k)
                        wh = slab_hi[:, s % RING, at + k * P:at + (k + 1) * P]
                        wl = slab_lo[:, s % RING, at + k * P:at + (k + 1) * P]
                        pe.matmul(out, wh, hi[:, k, half_cols(half)], start=k == 0, stop=False)
                        last = pe.matmul(out, wh, lo[:, k, half_cols(half)], start=False,
                                         stop=k == tiles - 1 and not lo_weights)
                        if lo_weights:
                            last = pe.matmul(out, wl, hi[:, k, half_cols(half)], start=False, stop=k == tiles - 1)
                    return last

                turn_attn(0)
                turn_attn(1)
                pe.wait_ge(slab_ready, c * SLABS + 2)
                for t in range(TT):
                    if t + 2 < TT:
                        turn_attn(t + 2)
                    pe.wait_ge(attn_lo_ready, c * 2 * TT + 2 * t + 2)
                    for half in range(2):
                        rows_out(t, half, half, at_hi, at_lo, True)
                    if t == TT - 2:
                        turn_y(0)
                        turn_y(1)
                pe.drain().then_inc(slab_used, 2)

                for n in range(UP_UNITS):
                    m, half = up_place(n)
                    s = SLAB_UP + m // 2
                    if n % 4 == 0:
                        pe.wait_ge(slab_ready, c * SLABS + s + 1)
                    if n == 0:
                        pe.wait_ge(y_lo_ready, c * (TT // 2) + 2)
                    if n == 2:
                        turn_y(2)
                        turn_y(3)
                        pe.wait_ge(y_lo_ready, c * (TT // 2) + 4)
                    if n >= 2:
                        pe.wait_ge(gated, c * UP_UNITS + n - 1)
                    for w in range(2):
                        last = product(ps_m[:, n % 2 * 2 + w, :], s, (m % 2 * 2 + w) * KD * P, y_hi, y_lo, half, KD)
                    last.then_inc(up_done, 1)
                    if n % 4 == 3:
                        pe.drain().then_inc(slab_used, 1)

                for n in range(HID_UNITS):
                    layer, m, half = hid_place(n)
                    s = SLAB_HID + layer * MT + m
                    if n % HALVES == 0:
                        pe.wait_ge(slab_ready, c * SLABS + s + 1)
                    if n < 2:
                        pe.wait_ge(gated, c * UP_UNITS + UP_UNITS - 1 + n)
                    elif n < 4:
                        pe.wait_ge(gated, (c + 1) * UP_UNITS)
                    else:
                        pe.wait_ge(gelu_ready, c * HID_UNITS + n - 3)

                    def inputs_ready(k):
                        if layer:
                            pe.wait_ge(hid_lo_ready, c * HID_UNITS + HALVES * k + half + 1)
                        else:
                            pe.wait_ge(up_lo_ready, c * UP_UNITS + up_units(k, half))

                    hi, lo = (hb_hi, hb_lo) if layer else (ha_hi, ha_lo)
                    product(ps_m[:, n % 4, :], s, 0, hi, lo, half, MT, inputs_ready if m == 0 else None) \
                        .then_inc(hid_done, 1)
                    if n % HALVES == HALVES - 1:
                        pe.drain().then_inc(slab_used, 1)

                for g in range(2):
                    for half in range(2):
                        if g == 0:
                            pe.wait_ge(slab_ready, c * SLABS + SLAB_DOWN + half + 1)
                        pe.wait_ge(hid_lo_ready, c * HID_UNITS + UP_UNITS + HALVES * (half * 4 + 3) + g + 1)
                        for t in range(g * HT, (g + 1) * HT):
                            rows_out(t, SLAB_DOWN + half, half, ha_hi, ha_lo, lo_weights)
                        if g == 1:
                            pe.drain().then_inc(slab_used, 1)

            pe.wait_ge(flag_step, 2)
            pe.matmul(ps_m[0:1, 0, 0:1], has_lo[:], ones[:], start=True, stop=True).then_inc(flag_step, 1)
            pe.wait_ge(consts_loaded, 16 * n_consts)
            pe.wait_ge(flag_step, 4)
            with_lo = pe.value_load(rows_with_lo[0:1, 0:1])
            with pe.If(with_lo > 0):
                with pe.Fori(0, CHUNKS) as c:
                    chunk(c, True)
            with pe.If(with_lo < 1):
                with pe.Fori(0, CHUNKS) as c:
                    chunk(c, False)


def program(nc, ins, out):
    attn_dram = nc.dram_tensor("attn_scratch", (B * NT + TT, P, H, DH), F32, kind="Internal").ap()
    with nc.sbuf_tensor("lo_max", [P, (B * PAIRS + PAIRS) * PIECES], F32) as lo_max:
        attention(nc, ins, attn_dram, lo_max)
        feed_forward(nc, ins, attn_dram, lo_max, out)


def _constants():
    import numpy as np

    pos = np.arange(S, dtype=np.float32)
    inv_freq = (1.0 / np.float32(10000.0) ** (np.arange(0, DH, 2, dtype=np.float32) / np.float32(DH))).astype(np.float32)
    freqs = np.outer(pos, inv_freq).astype(np.float32)
    rows = lambda a: np.ascontiguousarray(a.reshape(NT, P, -1).transpose(1, 0, 2)).astype(np.float32)
    start = 2.0 ** (-8.0 / H)
    slope = np.array([start ** (h + 1) for h in range(H)], np.float32) * np.float32(8.0)
    slopes = np.zeros(48, np.float32)
    slopes[0:2 * H] = np.tile(slope, 2)
    dist = np.arange(P)[:, None] - (np.arange(S)[None, :] - (S - P))
    return {
        "ident": np.eye(P, dtype=np.float32),
        "fold": np.concatenate([np.eye(DH, dtype=np.float32)] * 2),
        "cos": rows(np.cos(freqs)),
        "sin": rows(np.concatenate([-np.sin(freqs), np.sin(freqs)], axis=1)),
        "rel": np.maximum(dist, 0).astype(np.float16),
        "mask": np.where(dist[:, S - P:] < 0, np.float32(NEG_MASK), np.float32(0)).astype(np.float32),
        "slopes": np.ascontiguousarray(np.broadcast_to(slopes, (P, 48))),
    }


def kernel(L0_attn_x, L0_attn_w_qkv, L0_attn_b_qkv, L0_attn_w_out, L0_attn_b_out, L0_ffn_w1_w, L0_ffn_w1_s,
           L0_ffn_w2_w, L0_ffn_w2_s, L0_ffn_h1_w, L0_ffn_h1_s, L0_ffn_h2_w, L0_ffn_h2_s, L0_ffn_w3_w, L0_ffn_w3_s):
    import numpy as np
    import concourse.bacc as bacc
    from concourse.bass_utils import run_bass_kernel_spmd

    c = np.ascontiguousarray
    a = lambda v: np.asarray(v)

    def by_pair(w):
        w = w.reshape(w.shape[0], PAIRS, 2, 3, DH).transpose(1, 0, 3, 2, 4).reshape(PAIRS, w.shape[0], PAIR_COLS)
        return np.concatenate([w, w[0:1]])

    w_qkv = by_pair(a(L0_attn_w_qkv)).reshape(PAIRS + 1, KD, P, PAIR_COLS).transpose(0, 2, 1, 3)
    rows_k = lambda w: w.reshape(2, 4, P, DM).transpose(0, 2, 1, 3).reshape(2, P, SLAB)
    cols_m = lambda w: w.reshape(MT, P, -1, P).transpose(0, 3, 2, 1)
    up = np.stack([cols_m(a(L0_ffn_w1_w)), cols_m(a(L0_ffn_w2_w))], axis=2)
    up = up.reshape(MT // 2, 2, P, 2, KD, P).transpose(0, 2, 1, 3, 4, 5).reshape(MT // 2, P, SLAB)
    slabs = np.concatenate([
        rows_k(a(L0_attn_w_out).reshape(H * DH, DM)), up,
        cols_m(a(L0_ffn_h1_w)).reshape(MT, P, SLAB), cols_m(a(L0_ffn_h2_w)).reshape(MT, P, SLAB),
        rows_k(a(L0_ffn_w3_w).T),
    ])
    slabs = np.concatenate([slabs, slabs[-2:]])
    scales = np.stack([a(s).reshape(MT, P) for s in (L0_ffn_w1_s, L0_ffn_w2_s, L0_ffn_h1_s, L0_ffn_h2_s)])
    arrays = _constants() | {
        "x": a(L0_attn_x),
        "x_t": a(L0_attn_x).transpose(0, 2, 1).reshape(B, KD, P, S).transpose(0, 2, 1, 3),
        "w_qkv": w_qkv,
        "b_qkv": by_pair(a(L0_attn_b_qkv).reshape(1, H * 3 * DH)),
        "slabs": slabs,
        "s_hid": scales.transpose(2, 0, 1),
        "b_out": a(L0_attn_b_out).reshape(1, DM),
        "s_down": a(L0_ffn_w3_s).reshape(1, DM),
    }
    nc = bacc.Bacc("TRN2", target_bir_lowering=False, num_devices=1)
    feed, ins = {}, {}
    for name, v in arrays.items():
        feed[f"in_{name}"] = c(v)
        ins[name] = nc.dram_tensor(f"in_{name}", v.shape, mybir.dt.from_np(v.dtype), kind="ExternalInput").ap()
    out = nc.dram_tensor("out_rows", (B, S, DM), F32, kind="ExternalOutput").ap()
    program(nc, ins, out)
    return run_bass_kernel_spmd(nc, [feed], core_ids=[0]).results[0]["out_rows"]
```
